# Optimizing a Trainium2 kernel written in Bass

```python
import numpy as np
import jax
import jax.numpy as jnp

def _softmax(x, axis=-1):
    return jax.nn.softmax(x, axis=axis)

def _gelu(x):
    return jax.nn.gelu(x, approximate=True)

def _silu(x):
    return jax.nn.silu(x)

def _sigmoid(x):
    return jax.nn.sigmoid(x)

def _layernorm(x, axis=-1, eps=1e-05):
    m = jnp.mean(x, axis=axis, keepdims=True)
    v = jnp.var(x, axis=axis, keepdims=True)
    return (x - m) / jnp.sqrt(v + eps)

def _scatter_add(tgt, idx, src, axis=0):
    return tgt.at[idx].add(src)

def _segment_sum(src, seg, n):
    return jax.ops.segment_sum(src, seg, n)
kernel_name = 'mk_audio_tower_d1_tok_audfeat1024_r4_a0508b'

def setup_inputs(seed: int=0):
    np.random.seed(seed)
    _w = jnp.asarray

    def _rec_inputs():
        import jax
        import jax.numpy as jnp
        _rk = jax.random.key(seed)
        x = -0.000392918 + 0.999932 * jax.random.normal(jax.random.fold_in(_rk, 1), (64, 125, 256), jnp.float32)
        return x
    x = _rec_inputs()

    def _L0_tok_setup():
        import jax, jax.numpy as jnp
        import numpy as np
        D_MODEL = 256

        def _layernorm(h, gamma, beta, eps=1e-05):
            mu = jnp.mean(h, axis=-1, keepdims=True)
            var = jnp.mean(jnp.square(h - mu), axis=-1, keepdims=True)
            return (h - mu) * jax.lax.rsqrt(var + eps) * gamma + beta
        key = jax.random.key(seed)
        k_x, k_wd, k_wp, k_bp = jax.random.split(key, 4)
        d = D_MODEL
        x = jax.random.normal(k_x, (4, 1024, d), dtype=jnp.float32)
        Wd = jnp.eye(2 * d, dtype=jnp.float32) + 0.01 * jax.random.normal(k_wd, (2 * d, 2 * d), dtype=jnp.float32)
        bd = jnp.zeros((2 * d,), dtype=jnp.float32)
        bound = 1.0 / np.sqrt(2 * d)
        Wp = jax.random.uniform(k_wp, (d, 2 * d), dtype=jnp.float32, minval=-bound, maxval=bound)
        bp = jax.random.uniform(k_bp, (d,), dtype=jnp.float32, minval=-bound, maxval=bound)
        gamma = jnp.ones((d,), dtype=jnp.float32)
        beta = jnp.zeros((d,), dtype=jnp.float32)
        return {'x': x, 'Wd': Wd, 'bd': bd, 'Wp': Wp, 'bp': bp, 'gamma': gamma, 'beta': beta}
    _L0_tok_all = _L0_tok_setup()
    _L0_tok_in = {k: v for k, v in _L0_tok_all.items() if k in ('Wd', 'bd', 'Wp', 'bp', 'gamma', 'beta')}
    del _L0_tok_all

    def _L0_attn_setup():
        import jax, jax.numpy as jnp
        import numpy as np
        D_MODEL = 256
        N_HEADS = 16
        HEAD_DIM = D_MODEL // N_HEADS
        D_LATENT = 64
        LAMBDA_DECAY = 0.01
        TIME_STEP = 0.01
        CLAMP = 10000.0

        def _reference_tuple_inner(x, Wq, Wk, Wv, Wo, W_down_kv, W_up_k, W_up_v):
            B, S, _ = x.shape
            q = x @ Wq
            k = x @ Wk
            v = x @ Wv
            latent_kv = (k + v) @ W_down_kv
            k_rec = latent_kv @ W_up_k
            v_rec = latent_kv @ W_up_v

            def heads(t):
                return t.reshape(B, S, N_HEADS, HEAD_DIM).transpose(0, 2, 1, 3)
            qh, kh, vh = (heads(q), heads(k_rec), heads(v_rec))
            scale = 1.0 / (jnp.sqrt(jnp.float32(D_MODEL)) + 1e-08)
            scores = jnp.einsum('bhqd,bhkd->bhqk', qh, kh) * scale
            scores = jnp.clip(jnp.nan_to_num(scores, nan=-1000000000.0), -CLAMP, CLAMP)
            idx = jnp.arange(S, dtype=jnp.float32)
            decay = jnp.exp(-LAMBDA_DECAY * TIME_STEP * jnp.abs(idx[:, None] - idx[None, :]))
            scores = scores * decay[None, None, :, :]
            scores = jnp.clip(jnp.nan_to_num(scores, nan=-1000000000.0), -CLAMP, CLAMP)
            attn = jax.nn.softmax(scores, axis=-1)
            out = jnp.einsum('bhqk,bhkd->bhqd', attn, vh)
            out = out.transpose(0, 2, 1, 3).reshape(B, S, D_MODEL)
            return (out @ Wo, latent_kv)
        key = jax.random.key(seed)
        ks = jax.random.split(key, 8)
        B, S = (2, 512)

        def w(k, i, o):
            return jax.random.normal(k, (i, o), dtype=jnp.float32) * 0.02
        return {'x': jax.random.normal(ks[0], (B, S, D_MODEL), dtype=jnp.float32), 'Wq': w(ks[1], D_MODEL, D_MODEL), 'Wk': w(ks[2], D_MODEL, D_MODEL), 'Wv': w(ks[3], D_MODEL, D_MODEL), 'Wo': w(ks[4], D_MODEL, D_MODEL), 'W_down_kv': w(ks[5], D_MODEL, D_LATENT), 'W_up_k': w(ks[6], D_LATENT, D_MODEL), 'W_up_v': w(ks[7], D_LATENT, D_MODEL)}
    _L0_attn_all = _L0_attn_setup()
    _L0_attn_in = {k: v for k, v in _L0_attn_all.items() if k in ('Wq', 'Wk', 'Wv', 'Wo', 'W_down_kv', 'W_up_k', 'W_up_v')}
    del _L0_attn_all

    def _L0_ffn_setup():
        import jax, jax.numpy as jnp
        import numpy as np
        B, S, D, F, E = (4, 512, 256, 1024, 4)
        key = jax.random.key(seed)
        ks = jax.random.split(key, 8)
        sd = 1.0 / np.sqrt(D)
        sf = 1.0 / np.sqrt(F)
        return {'x': jax.random.normal(ks[0], (B, S, D), dtype=jnp.float32), 'W1': jax.random.uniform(ks[1], (E, D, F), jnp.float32, -sd, sd), 'b1': jax.random.uniform(ks[2], (E, F), jnp.float32, -sd, sd), 'W2': jax.random.uniform(ks[3], (E, F, D), jnp.float32, -sf, sf), 'b2': jax.random.uniform(ks[4], (E, D), jnp.float32, -sf, sf), 'Wu': jax.random.uniform(ks[5], (D, 1), jnp.float32, -sd, sd), 'bu': jax.random.uniform(ks[6], (1,), jnp.float32, -sd, sd)}
    _L0_ffn_all = _L0_ffn_setup()
    _L0_ffn_in = {k: v for k, v in _L0_ffn_all.items() if k in ('W1', 'b1', 'W2', 'b2', 'Wu', 'bu')}
    del _L0_ffn_all
    return {'x': x, 'L0_tok_Wd': _L0_tok_in['Wd'], 'L0_tok_bd': _L0_tok_in['bd'], 'L0_tok_Wp': _L0_tok_in['Wp'], 'L0_tok_bp': _L0_tok_in['bp'], 'L0_tok_gamma': _L0_tok_in['gamma'], 'L0_tok_beta': _L0_tok_in['beta'], 'L0_attn_Wq': _L0_attn_in['Wq'], 'L0_attn_Wk': _L0_attn_in['Wk'], 'L0_attn_Wv': _L0_attn_in['Wv'], 'L0_attn_Wo': _L0_attn_in['Wo'], 'L0_attn_W_down_kv': _L0_attn_in['W_down_kv'], 'L0_attn_W_up_k': _L0_attn_in['W_up_k'], 'L0_attn_W_up_v': _L0_attn_in['W_up_v'], 'L0_ffn_W1': _L0_ffn_in['W1'], 'L0_ffn_b1': _L0_ffn_in['b1'], 'L0_ffn_W2': _L0_ffn_in['W2'], 'L0_ffn_b2': _L0_ffn_in['b2'], 'L0_ffn_Wu': _L0_ffn_in['Wu'], 'L0_ffn_bu': _L0_ffn_in['bu']}

def reference(x, L0_tok_Wd, L0_tok_bd, L0_tok_Wp, L0_tok_bp, L0_tok_gamma, L0_tok_beta, L0_attn_Wq, L0_attn_Wk, L0_attn_Wv, L0_attn_Wo, L0_attn_W_down_kv, L0_attn_W_up_k, L0_attn_W_up_v, L0_ffn_W1, L0_ffn_b1, L0_ffn_W2, L0_ffn_b2, L0_ffn_Wu, L0_ffn_bu):
    import jax
    import jax.numpy as jnp

    def _L0_tok_ref(x, Wd, bd, Wp, bp, gamma, beta):
        import jax, jax.numpy as jnp
        import numpy as np
        D_MODEL = 256

        def _layernorm(h, gamma, beta, eps=1e-05):
            mu = jnp.mean(h, axis=-1, keepdims=True)
            var = jnp.mean(jnp.square(h - mu), axis=-1, keepdims=True)
            return (h - mu) * jax.lax.rsqrt(var + eps) * gamma + beta
        B, T, d = x.shape
        T2 = T // 2 * 2
        x = x[:, :T2, :]
        pair = jnp.concatenate([x[:, 0::2, :], x[:, 1::2, :]], axis=-1)
        h = jnp.tanh(jnp.einsum('btf,gf->btg', pair, Wd) + bd)
        y = jnp.einsum('btg,dg->btd', h, Wp) + bp
        return _layernorm(y, gamma, beta)

    def _L0_attn_ref(x, Wq, Wk, Wv, Wo, W_down_kv, W_up_k, W_up_v):
        import jax, jax.numpy as jnp
        import numpy as np
        D_MODEL = 256
        N_HEADS = 16
        HEAD_DIM = D_MODEL // N_HEADS
        D_LATENT = 64
        LAMBDA_DECAY = 0.01
        TIME_STEP = 0.01
        CLAMP = 10000.0

        def _reference_tuple_inner(x, Wq, Wk, Wv, Wo, W_down_kv, W_up_k, W_up_v):
            B, S, _ = x.shape
            q = x @ Wq
            k = x @ Wk
            v = x @ Wv
            latent_kv = (k + v) @ W_down_kv
            k_rec = latent_kv @ W_up_k
            v_rec = latent_kv @ W_up_v

            def heads(t):
                return t.reshape(B, S, N_HEADS, HEAD_DIM).transpose(0, 2, 1, 3)
            qh, kh, vh = (heads(q), heads(k_rec), heads(v_rec))
            scale = 1.0 / (jnp.sqrt(jnp.float32(D_MODEL)) + 1e-08)
            scores = jnp.einsum('bhqd,bhkd->bhqk', qh, kh) * scale
            scores = jnp.clip(jnp.nan_to_num(scores, nan=-1000000000.0), -CLAMP, CLAMP)
            idx = jnp.arange(S, dtype=jnp.float32)
            decay = jnp.exp(-LAMBDA_DECAY * TIME_STEP * jnp.abs(idx[:, None] - idx[None, :]))
            scores = scores * decay[None, None, :, :]
            scores = jnp.clip(jnp.nan_to_num(scores, nan=-1000000000.0), -CLAMP, CLAMP)
            attn = jax.nn.softmax(scores, axis=-1)
            out = jnp.einsum('bhqk,bhkd->bhqd', attn, vh)
            out = out.transpose(0, 2, 1, 3).reshape(B, S, D_MODEL)
            return (out @ Wo, latent_kv)
        return _reference_tuple_inner(x, Wq, Wk, Wv, Wo, W_down_kv, W_up_k, W_up_v)[0]

    def _L0_ffn_ref(x, W1, b1, W2, b2, Wu, bu):
        import jax, jax.numpy as jnp
        import numpy as np
        B, S, D, F, E = (4, 512, 256, 1024, 4)
        n_exp = W1.shape[0]
        seq = x.shape[1]
        u = jax.nn.sigmoid(jnp.einsum('bsd,do->bso', x, Wu) + bu)[..., 0]
        k = jnp.clip(jnp.ceil(u * n_exp), 1, n_exp).astype(jnp.int32)
        h = jax.nn.relu(jnp.einsum('bsd,edf->bsef', x, W1) + b1)
        y = jnp.einsum('bsef,efd->bsed', h, W2) + b2
        s_idx = jnp.arange(seq)
        out = jnp.zeros_like(x)
        for i in range(1, n_exp + 1):
            e_idx = (s_idx + i - 1) % n_exp
            y_i = jnp.take_along_axis(y, e_idx[None, :, None, None], axis=2)[:, :, 0, :]
            w = jnp.where(k >= i, u / i, 0.0)
            out = out + w[..., None] * y_i
        return out
    h = _L0_tok_ref(x, L0_tok_Wd, L0_tok_bd, L0_tok_Wp, L0_tok_bp, L0_tok_gamma, L0_tok_beta)
    h = h + _L0_attn_ref(_layernorm(h, axis=-1), L0_attn_Wq, L0_attn_Wk, L0_attn_Wv, L0_attn_Wo, L0_attn_W_down_kv, L0_attn_W_up_k, L0_attn_W_up_v)
    h = h + _L0_ffn_ref(_layernorm(h, axis=-1), L0_ffn_W1, L0_ffn_b1, L0_ffn_W2, L0_ffn_b2, L0_ffn_Wu, L0_ffn_bu)
    return h

_drawn_inputs = setup_inputs


def setup_inputs(seed=0):
    import zlib

    import numpy as np

    out = dict(_drawn_inputs(seed))
    spreads = {'L0_tok_bd': (0.0, 0.1), 'L0_tok_gamma': (1.0, 0.2), 'L0_tok_beta': (0.0, 0.1)}
    factors = {'L0_attn_Wq': 8.0,
     'L0_attn_Wk': 8.0,
     'L0_attn_Wv': 8.0,
     'L0_attn_Wo': 8.0,
     'L0_attn_W_down_kv': 8.0,
     'L0_attn_W_up_k': 8.0,
     'L0_attn_W_up_v': 8.0,
     'L0_ffn_b1': 52.056,
     'L0_ffn_b2': 44.28,
     'L0_ffn_W1': 8.0,
     'L0_ffn_W2': 8.0,
     'L0_ffn_Wu': 8.0}
    for name, (base, spread) in spreads.items():
        noise = np.random.default_rng([zlib.crc32(name.encode()), seed]).standard_normal(out[name].shape)
        drawn = base * np.exp(spread * noise) if base else spread * noise
        out[name] = jnp.asarray(drawn.astype(out[name].dtype))
    for name, factor in factors.items():
        out[name] = (out[name] * factor).astype(out[name].dtype)
    return out
```

```python
from contextlib import ExitStack

import concourse.bass as bass
from concourse import mybir

F32 = mybir.dt.float32
F32R = mybir.dt.float32r
ALU = mybir.AluOpType
ACT = mybir.ActivationFunctionType
AX = mybir.AxisListType

P = 128
CLIPS, FRAMES, D = 64, 125, 256
S = FRAMES // 2
HALF = 64
TILES = CLIPS // 2
ROWS = 2 * S
F2D = 2 * D
HEADS, DH, LAT = 16, 16, 64
QUADS, HPQ = 4, 4
FF, EXPERTS = 1024, 4
KD, KF, KT = D // P, F2D // P, FF // P
CHUNKS, TPC = 8, TILES // 8
CW = TPC * ROWS
LN_EPS = 1e-5
CLAMP = 10000.0
SCALE_INV = 16.0
LAST_LAG = 4
WCOLS = KD * FF
PREP = 2 * WCOLS // CHUNKS


def build(nc, x, Wd, bd, Wp, bp, gamma, beta, Wq, Wk, Wv, Wo, Wdown, Wupk, Wupv,
          W1, b1, W2, b2, Wu, bu, c_ident, c_decay, c_headmask, c_gate, out):
    ctx = ExitStack()
    with ctx:
        def sem(name):
            return ctx.enter_context(nc.semaphore(name))

        def sb(name, shape, dt=F32, stack=None):
            return (stack or ctx).enter_context(nc.sbuf_tensor(name, shape, dt))

        x2_hi = sb("x2_hi", [P, KD, TILES * ROWS], F32R)
        x2_lo = sb("x2_lo", [P, KD, TILES * ROWS], F32R)
        resid = sb("resid", [P, TILES, D])
        we_hi = [sb("we_hi0", [P, 2 * WCOLS], F32R)]
        we_lo = [sb("we_lo0", [P, 2 * WCOLS], F32R)]
        ident = sb("ident_sb", [P, P])
        b12T = sb("b12T", [P, EXPERTS * KT + EXPERTS * KD])
        gate = sb("gate", [P, 2 * EXPERTS])
        logit = sb("logit", [P, TILES])
        logit_one = sb("logit_one", [P, 1])
        u_exp = sb("u_exp", [P, TILES])
        u_den = sb("u_den", [P, TILES])
        u = sb("u", [P, TILES])
        neg_bu = sb("neg_bu", [P, 1])
        w_step = sb("w_step", [P, EXPERTS, TILES])
        w_gate = sb("w_gate", [P, EXPERTS, TILES])
        psum = ctx.enter_context(nc.psum_tensor("psum", [P, 8, 512], F32))

        scratch = resid[:, :, :].rearrange("p t d -> p (t d)")
        used = [0]

        def stage(cols):
            used[0] += cols
            return scratch[:, used[0] - cols:used[0]]

        wd_raw = stage(KF * F2D).rearrange("p (a b) -> p a b", a=KF)
        wp_raw = stage(KD * F2D).rearrange("p (a b) -> p a b", a=KD)
        wk_raw = stage(KD * D)
        wv_raw = stage(KD * D)
        wkv = stage(KD * D).rearrange("p (a b) -> p a b", a=KD)
        wkvT = stage(KD * D).rearrange("p (a b) -> p a b", a=KD)
        wdown = stage(KD * LAT).rearrange("p (a b) -> p a b", a=KD)
        b12_raw = stage(P)
        we_raw0 = stage(WCOLS)
        bias_raw = stage(F2D + D)
        assert used[0] <= TILES * D

        pa = ExitStack()
        wdT_hi = sb("wdT_hi", [P, KF, F2D], F32R, pa)
        wdT_lo = sb("wdT_lo", [P, KF, F2D], F32R, pa)
        wpT_hi = sb("wpT_hi", [P, KF, D], F32R, pa)
        wpT_lo = sb("wpT_lo", [P, KF, D], F32R, pa)
        wq = sb("wq", [P, KD, D], stack=pa)
        wo = sb("wo", [P, KD, D], stack=pa)
        wkvd = sb("wkvd", [P, KD, LAT], stack=pa)
        wup = sb("wup", [LAT, 2 * D], stack=pa)
        bias2 = sb("bias2", [P, F2D + D], F32R, pa)
        ones = sb("ones", [P, P], F32R, pa)
        gamma_b = sb("gamma_b", [P, D], stack=pa)
        beta_b = sb("beta_b", [P, D], stack=pa)
        wu_b = sb("wu_b", [P, D], stack=pa)
        decay = sb("decay", [P, S], stack=pa)
        headmask = sb("headmask", [P, HPQ], stack=pa)
        neg_half = sb("neg_half", [P, 1], stack=pa)
        eps = sb("eps", [P, 1], stack=pa)
        tick = sb("tick", [P, 1], stack=pa)
        x_sb = sb("x_sb", [P, F2D], stack=pa)
        xT_hi = sb("xT_hi", [P, KF, P], F32R, pa)
        xT_lo = sb("xT_lo", [P, KF, P], F32R, pa)
        hid = sb("hid", [P, F2D], stack=pa)
        hidT_hi = sb("hidT_hi", [P, KF, P], F32R, pa)
        hidT_lo = sb("hidT_lo", [P, KF, P], F32R, pa)
        y_stats = sb("y_stats", [P, 6], stack=pa)
        y_mv = sb("y_mv", [P, 2], stack=pa)
        y_ve = sb("y_ve", [P, 1], stack=pa)
        y_rstd = sb("y_rstd", [P, 1], stack=pa)
        h0_stats = sb("h0_stats", [P, 6], stack=pa)
        h0_mv = sb("h0_mv", [P, 2], stack=pa)
        h0_ve = sb("h0_ve", [P, 1], stack=pa)
        h0_rstd = sb("h0_rstd", [P, 1], stack=pa)
        h1_stats = sb("h1_stats", [P, 6], stack=pa)
        h1_mv = sb("h1_mv", [P, 2], stack=pa)
        h1_ve = sb("h1_ve", [P, 1], stack=pa)
        h1_rstd = sb("h1_rstd", [P, 1], stack=pa)
        xn = sb("xn", [P, D], stack=pa)
        xnT = sb("xnT", [P, KD, P], stack=pa)
        latT = sb("latT", [LAT, P], stack=pa)
        q_bd = sb("q_bd", [P, QUADS, P], stack=pa)
        k_cp = sb("k_cp", [P, QUADS, S], stack=pa)
        k_exp = sb("k_exp", [P, QUADS, HPQ, S], stack=pa)
        v_bd = sb("v_bd", [P, HEADS // 2, 2, 2, DH], stack=pa)
        shifted = sb("shifted", [P, HEADS, S], stack=pa)
        row_max = sb("row_max", [P, HEADS], stack=pa)
        row_sum = sb("row_sum", [P, HEADS], stack=pa)
        row_inv = sb("row_inv", [P, HEADS], stack=pa)
        probs = sb("probs", [P, HEADS, HALF], stack=pa)
        pT = sb("pT", [P, HEADS // 2, P], stack=pa)
        o_sb = sb("o_sb", [P, HEADS, DH], stack=pa)
        oT = sb("oT", [P, KD, P], stack=pa)
        xn2 = sb("xn2", [P, D], stack=pa)
        logit_terms = sb("logit_terms", [P, D], stack=pa)
        pa.close()

        pb = ExitStack()
        we_hi.append(sb("we_hi1", [P, 2 * WCOLS], F32R, pb))
        we_lo.append(sb("we_lo1", [P, 2 * WCOLS], F32R, pb))
        we_raw = sb("we_raw", [P, 2 * WCOLS], stack=pb)
        h_full = sb("h_full", [P, 2, CW], stack=pb)
        h_hi = sb("h_hi", [P, 4, CW], F32R, pb)
        h_lo = sb("h_lo", [P, 4, CW], F32R, pb)
        y_sb = sb("y_sb", [P, KD, 2 * TPC, HALF], stack=pb)
        pb.close()

        bk_x, bk_s, bk_p, bk_m, bk_h, bk_q, bk_o = 0, 1, 3, 4, 5, 6, 7
        ps_xT = psum[:, bk_x, :].rearrange("p (k c) -> p k c", k=KF)
        ps_sc = psum[:, bk_s:bk_s + 2, 0:2 * HPQ * S]
        ps_sc_h = ps_sc.rearrange("p b (h k) -> p b h k", k=S)
        ps_pT = psum[:, bk_p:bk_p + 2, :]
        ps_x2T = psum[:, bk_p, 0:KD * P]
        ps_oT = psum[:, bk_p, 0:KD * P]
        ps_v = psum[:, bk_m, 0:D]
        ps_at = psum[:, bk_m, 0:D]
        ps_h = psum[:, bk_h, :]
        ps_y = psum[:, bk_h, 0:D]
        ps_xnT = psum[:, bk_q, 0:KD * P]
        ps_q = psum[:, bk_q, 0:KD * P].rearrange("p (m c) -> p m c", m=KD)
        ps_lat = psum[0:LAT, bk_q, KD * P:KD * P + P]
        ps_k = psum[:, bk_o, 0:KD * P].rearrange("p (m c) -> p m c", m=KD)
        ps_pv = psum[:, bk_o, :].rearrange("p (h b e d) -> p h b e d", h=HEADS // 2, b=2, e=2)
        bk_f1, bk_y, bk_t = 0, 3, 5
        ps_yT = psum[:, bk_t:bk_t + 2, :].rearrange("p b (j d) -> p (b j) d", j=2)

        ld_tok, ld_att, ld_small, ld_b12, ld_up = (sem(s) for s in ("ld_tok", "ld_att", "ld_small", "ld_b12", "ld_up"))
        ld_bias, ld_we0, ld_we = sem("ld_bias"), sem("ld_we0"), sem("ld_we")
        zeroed, wkv_sum, setup_pe, setup_hi, setup_lo = (sem(s) for s in ("zeroed", "wkv_sum", "setup_pe", "setup_hi", "setup_lo"))
        bias_h, bias_done, we0_hi, we0_lo = sem("bias_h"), sem("bias_done"), sem("we0_hi"), sem("we0_lo")
        x_loaded = sem("x_loaded")
        x_turned, xT_hi_ok, xT_lo_ok, hid_sum = sem("x_turned"), sem("xT_hi_ok"), sem("xT_lo_ok"), sem("hid_sum")
        hid_ok, hid_turned, hidT_hi_ok, hidT_lo_ok = sem("hid_ok"), sem("hid_turned"), sem("hidT_hi_ok"), sem("hidT_lo_ok")
        y_sum, y_st_ok, y_mv_ok, y_ve_ok, y_rstd_ok = (sem(s) for s in ("y_sum", "y_st_ok", "y_mv_ok", "y_ve_ok", "y_rstd_ok"))
        y_normed, y_scaled, h0_ok = sem("y_normed"), sem("y_scaled"), sem("h0_ok")
        h0_st_ok, h0_mv_ok, h0_ve_ok, h0_rstd_ok = sem("h0_st_ok"), sem("h0_mv_ok"), sem("h0_ve_ok"), sem("h0_rstd_ok")
        xn_ok, xn_turned, xnT_ok, q_sum = sem("xn_ok"), sem("xn_turned"), sem("xnT_ok"), sem("q_sum")
        lat_ok, q_ok, k_sum, k_cp_ok, k_exp_ok = (sem(s) for s in ("lat_ok", "q_ok", "k_sum", "k_cp_ok", "k_exp_ok"))
        v_sum, v_ok = sem("v_sum"), sem("v_ok")
        sc_sum, sc_clipped, sc_decayed, max_ok, sc_shifted = (sem(s) for s in ("sc_sum", "sc_clipped", "sc_decayed", "max_ok", "sc_shifted"))
        probs_ok, sum_ok, inv_ok, p_turned, pT_ok = (sem(s) for s in ("probs_ok", "sum_ok", "inv_ok", "p_turned", "pT_ok"))
        pv_sum, o_ok, o_turned, oT_ok, at_sum = (sem(s) for s in ("pv_sum", "o_ok", "o_turned", "oT_ok", "at_sum"))
        h1_ok, h1_st_ok, h1_mv_ok, h1_ve_ok, h1_rstd_ok = (sem(s) for s in ("h1_ok", "h1_st_ok", "h1_mv_ok", "h1_ve_ok", "h1_rstd_ok"))
        xn2_ok, xn2_turned, x2_hi_ok, x2_lo_ok, logit_ok = (sem(s) for s in ("xn2_ok", "xn2_turned", "x2_hi_ok", "x2_lo_ok", "logit_ok"))
        logit_one_ok = sem("logit_one_ok")
        g_exp, g_step, w_ok = sem("g_exp"), sem("g_step"), sem("w_ok")
        f1_sum, h_ok, h_hi_ok, h_lo_ok, f2_sum = (sem(s) for s in ("f1_sum", "h_ok", "h_hi_ok", "h_lo_ok", "f2_sum"))
        y_pad, ye_ok, ye_turned, acc_ok = sem("y_pad"), sem("ye_ok"), sem("ye_turned"), sem("acc_ok")
        we_hi_ok, we_lo_ok, stored = sem("we_hi_ok"), sem("we_lo_ok"), sem("stored")

        N_SPLIT = KF + KF // 2

        def runs(n, lag):
            return not isinstance(n, int) or 0 <= n - lag < TILES

        def wait(eng, s, n, more=0, each=1):
            if isinstance(n, int):
                count = min(n + more, TILES) * each
                if count > 0:
                    eng.wait_ge(s, count)
            else:
                eng.wait_ge(s, (n + more) * each)

        def tile_rows(t):
            return resid[:, bass.ds(t, 1), :].rearrange("p t d -> p (t d)")

        def steps(eng, step):
            for n in range(LAST_LAG + 1):
                step(n)
            with eng.Fori(LAST_LAG + 1, TILES) as n:
                step(n)
            for n in range(TILES, TILES + LAST_LAG):
                step(n)

        def chunks(eng, chunk):
            for e in range(EXPERTS):
                if e == 0:
                    chunk(0, 0)
                with eng.Fori(1 if e == 0 else 0, CHUNKS) as c:
                    chunk(e, c)

        block = ctx.enter_context(nc.Block())

        @block.sync
        def _(sp):
            for t in range(2):
                sp.dma_start(wd_raw[:, 2 * t:2 * t + 2, :], Wd.rearrange("(a p) f -> p a f", p=P)[:, 2 * t:2 * t + 2, :]).then_inc(ld_tok, 16)
            sp.dma_start(ident[:, :], c_ident).then_inc(ld_small, 16)
            sp.dma_start(wp_raw, Wp.rearrange("(a p) f -> p a f", p=P)).then_inc(ld_tok, 16)
            sp.wait_ge(zeroed, 1)

            def load_x(n):
                if not runs(n, 0):
                    return
                wait(sp, x_turned, n)
                for half in range(2):
                    rows = x[bass.ds(2 * n + half, 1), 0:2 * S, :].rearrange("a (t j) d -> (a t) (j d)", j=2)
                    for a, b in ((0, 48), (48, S)):
                        sp.dma_start(x_sb[HALF * half + a:HALF * half + b, :], rows[a:b, :]).then_inc(x_loaded, 16)

            load_x(0)
            for row in (0, 32):
                sp.dma_start(bias_raw[row:row + 1, 0:F2D], bd.rearrange("(a d) -> a d", a=1)).then_inc(ld_bias, 16)
                sp.dma_start(bias_raw[row:row + 1, F2D:], bp.rearrange("(a d) -> a d", a=1)).then_inc(ld_bias, 16)
            for src, dst in ((Wk, wk_raw), (Wv, wv_raw), (Wdown, wdown), (Wq, wq), (Wo, wo)):
                d = dst if len(dst.shape) == 3 else dst.rearrange("p (a b) -> p a b", a=KD)
                sp.dma_start(d[:, :, :], src.rearrange("(a p) f -> p a f", p=P)).then_inc(ld_att, 16)
            sp.dma_start(wup[:, 0:D], Wupk).then_inc(ld_up, 16)
            sp.dma_start(wup[:, D:], Wupv).then_inc(ld_up, 16)
            sp.dma_start(b12_raw[0:EXPERTS * KT, :], b1.rearrange("e (f p) -> (e f) p", p=P)).then_inc(ld_b12, 16)
            sp.dma_start(b12_raw[EXPERTS * KT:EXPERTS * (KT + KD), :], b2.rearrange("e (f p) -> (e f) p", p=P)).then_inc(ld_b12, 16)
            sp.dma_start(gamma_b[:, :], gamma.partition_broadcast(P)).then_inc(ld_small, 16)
            sp.dma_start(beta_b[:, :], beta.partition_broadcast(P)).then_inc(ld_small, 16)
            sp.dma_start(wu_b[:, :], Wu.rearrange("d o -> (d o)").partition_broadcast(P)).then_inc(ld_small, 16)
            sp.dma_start(neg_bu[:, :], bu.partition_broadcast(P)).then_inc(ld_small, 16)
            sp.dma_start(decay[:, :], c_decay).then_inc(ld_small, 16)
            sp.dma_start(headmask[:, :], c_headmask).then_inc(ld_small, 16)
            sp.dma_start(gate[:, :], c_gate).then_inc(ld_small, 16)
            sp.dma_start(we_raw0.rearrange("p (k f) -> p k f", k=KD), W1[0].rearrange("(k p) f -> p k f", p=P)).then_inc(ld_we0, 16)

            def step(n):
                if isinstance(n, int) and n == 0:
                    return
                load_x(n)
                if isinstance(n, int) and n == 1:
                    sp.wait_ge(we0_lo, 1)
                    sp.dma_start(we_raw0.rearrange("p (k f) -> p k f", k=KT), W2[0].rearrange("(k p) f -> p k f", p=P)).then_inc(ld_we0, 16)

            steps(sp, step)
            sp.wait_ge(w_ok, 1)
            sp.wait_ge(oT_ok, TILES)
            sp.wait_ge(at_sum, TILES)
            sp.wait_ge(xn2_turned, TILES)
            for e in range(1, EXPERTS):
                if e > 1:
                    sp.wait_ge(we_lo_ok, CHUNKS * (e - 1))
                sp.dma_start(we_raw[:, 0:WCOLS].rearrange("p (k f) -> p k f", k=KD), W1[e].rearrange("(k p) f -> p k f", p=P)).then_inc(ld_we, 16)
                sp.dma_start(we_raw[:, WCOLS:].rearrange("p (k f) -> p k f", k=KT), W2[e].rearrange("(k p) f -> p k f", p=P)).then_inc(ld_we, 16)
            with sp.Fori(0, CHUNKS) as c:
                sp.wait_ge(acc_ok, c + ((EXPERTS - 1) * CHUNKS + 2))
                for half in range(2):
                    for j in range(TPC):
                        o = out[bass.ds(2 * TPC * c + (2 * j + half), 1), :, :].rearrange("a t d -> (a t) d")
                        r = resid[:, bass.ds(TPC * c + j, 1), :].rearrange("p t d -> p (t d)")
                        for a, b in ((0, 48), (48, S)):
                            sp.dma_start(o[a:b, :], r[HALF * half + a:HALF * half + b, :]).then_inc(stored, 16)
            sp.wait_ge(stored, 16 * 4 * TILES)

        @block.gpsimd
        def _(pool):
            nc.gpsimd.memset(x_sb[:, :], 0.0).then_inc(zeroed, 1)
            nc.gpsimd.memset(bias2[:, :].bitcast(F32), 0.0).then_inc(zeroed, 1)
            nc.gpsimd.memset(ones[:, :].bitcast(F32), 1.0).then_inc(zeroed, 1)
            nc.gpsimd.memset(neg_half[:, :], -0.5).then_inc(zeroed, 1)
            nc.gpsimd.memset(eps[:, :], LN_EPS).then_inc(zeroed, 1)
            nc.gpsimd.memset(probs[:, :, :], 0.0).then_inc(zeroed, 1)
            nc.gpsimd.memset(q_bd[:, :, :], 0.0).then_inc(zeroed, 1)
            nc.gpsimd.memset(v_bd[:, :, :, :, :], 0.0).then_inc(zeroed, 1)
            pool.wait_ge(ld_small, 8 * 16)

            def rstd(n, mv, mv_ok, ve, ve_ok, r, r_ok):
                wait(pool, mv_ok, n, 1)
                nc.gpsimd.tensor_tensor(ve[:, :], mv[:, 1:2], eps[:, :], ALU.add).then_inc(ve_ok, 1)
                wait(pool, ve_ok, n, 1)
                nc.gpsimd.tensor_tensor(r[:, :], ve[:, :], neg_half[:, :], ALU.pow).then_inc(r_ok, 1)

            def pause():
                nc.gpsimd.tensor_tensor(tick[:, :], eps[:, :], eps[:, :], ALU.add)

            def step(n):
                if runs(n, 1):
                    h = tile_rows(n - 1)
                    wait(pool, y_normed, n - 1, 1)
                    pause()
                    nc.gpsimd.tensor_tensor(h, h, gamma_b[:, :], ALU.mult).then_inc(y_scaled, 1)
                    wait(pool, y_scaled, n - 1, 1)
                    pause()
                    nc.gpsimd.tensor_tensor(h, h, beta_b[:, :], ALU.add).then_inc(h0_ok, 1)
                if runs(n, 4):
                    rstd(n - 4, h1_mv, h1_mv_ok, h1_ve, h1_ve_ok, h1_rstd, h1_rstd_ok)
                if runs(n, 1):
                    rstd(n - 1, h0_mv, h0_mv_ok, h0_ve, h0_ve_ok, h0_rstd, h0_rstd_ok)
                    wait(pool, k_cp_ok, n - 1, 1)
                    wait(pool, sc_sum, n - 1)
                    nc.gpsimd.tensor_tensor(
                        k_exp[:, :, :, :],
                        k_cp[:, :, :].unsqueeze(2).broadcast_to([P, QUADS, HPQ, S]),
                        headmask[:, :].unsqueeze(1).unsqueeze(3).broadcast_to([P, QUADS, HPQ, S]),
                        ALU.mult).then_inc(k_exp_ok, 1)
                if runs(n, 0):
                    rstd(n, y_mv, y_mv_ok, y_ve, y_ve_ok, y_rstd, y_rstd_ok)
                if isinstance(n, int) and n < 2:
                    part = slice(n * WCOLS, (n + 1) * WCOLS)
                    pool.wait_ge(we0_hi, n + 1)
                    nc.gpsimd.tensor_tensor(we_lo[0][:, part], we_raw0, we_hi[0][:, part].bitcast(F32),
                                            ALU.subtract).then_inc(we0_lo, 1)

            steps(pool, step)
            pool.wait_ge(w_ok, 1)
            pool.wait_ge(oT_ok, TILES)
            pool.wait_ge(at_sum, TILES)
            pool.wait_ge(xn2_turned, TILES)
            nc.gpsimd.memset(y_sb[:, :, :, :], 0.0).then_inc(y_pad, 1)
            for e in range(1, EXPERTS):
                with pool.Fori(0, CHUNKS) as c:
                    part = bass.ds(PREP * c, PREP)
                    pool.wait_ge(we_hi_ok, c + (CHUNKS * (e - 1) + 1))
                    nc.gpsimd.tensor_tensor(we_lo[e % 2][:, part], we_raw[:, part],
                                            we_hi[e % 2][:, part].bitcast(F32), ALU.subtract).then_inc(we_lo_ok, 1)

        @block.scalar
        def _(act):
            for k in range(N_SPLIT):
                act.wait_ge(setup_pe, k + 1)
                if k < KF:
                    dst = wdT_hi[:, k, :]
                else:
                    dst = wpT_hi[:, 2 * (k - KF):2 * (k - KF) + 2, :].rearrange("p a d -> p (a d)")
                nc.scalar.activation(dst, psum[:, k, :], ACT.Copy).then_inc(setup_hi, 1)
            act.wait_ge(zeroed, 8)
            act.wait_ge(ld_bias, 64)
            nc.scalar.activation(bias2[0:1, :], bias_raw[0:1, :], ACT.Copy).then_inc(bias_h, 1)
            act.wait_ge(setup_pe, N_SPLIT + 1)
            nc.scalar.activation(wkvT[:, :, :].rearrange("p a b -> p (a b)"), psum[:, 6, :], ACT.Copy).then_inc(setup_hi, 1)
            nc.scalar.activation(b12T[:, :], psum[:, 7, 0:EXPERTS * (KT + KD)], ACT.Copy).then_inc(setup_hi, 1)
            act.wait_ge(setup_pe, N_SPLIT + 2)
            nc.scalar.activation(wkvd[:, :, :].rearrange("p a b -> p (a b)"), psum[:, 7, 128:128 + KD * LAT], ACT.Copy).then_inc(setup_hi, 1)

            def step(n):
                if runs(n, 0):
                    wait(act, x_turned, n, 1)
                    wait(act, hid_sum, n)
                    nc.scalar.activation(xT_hi[:, :, :], ps_xT, ACT.Copy).then_inc(xT_hi_ok, 1)
                if runs(n, 3):
                    wait(act, p_turned, n - 3, 1)
                    wait(act, pv_sum, n - 3)
                    for b in range(2):
                        last = nc.scalar.activation(pT[:, 4 * b:4 * b + 4, :].rearrange("p h q -> p (h q)"),
                                                    ps_pT[:, b, :], ACT.Copy)
                    last.then_inc(pT_ok, 1)
                if runs(n, 0):
                    wait(act, hid_sum, n, 1)
                    wait(act, hid_turned, n)
                    nc.scalar.activation(hid[:, :], ps_h, ACT.Tanh).then_inc(hid_ok, 1)
                if runs(n, 4):
                    wait(act, xn2_turned, n - 4, 1)
                    nc.scalar.activation(
                        x2_hi[:, :, bass.ds(ROWS * (n - 4), ROWS)].rearrange("p k (b t) -> p k b t", b=2),
                        ps_x2T.rearrange("p (k b t) -> p k b t", k=KD, b=2)[:, :, :, 0:S], ACT.Copy).then_inc(x2_hi_ok, 1)
                if runs(n, 1):
                    wait(act, xn_turned, n - 1, 1)
                    wait(act, q_sum, n - 1)
                    nc.scalar.activation(xnT[:, :, :].rearrange("p k c -> p (k c)"), ps_xnT, ACT.Copy).then_inc(xnT_ok, 1)
                if runs(n, 2):
                    wait(act, v_sum, n - 2, 1)
                    wait(act, pv_sum, n - 2)
                    pv = ps_v.rearrange("p (h e d) -> p h e d", h=HEADS // 2, e=2)
                    for clip in range(2):
                        for par in range(2):
                            last = nc.scalar.activation(
                                v_bd[HALF * par:HALF * (par + 1), :, clip, par, :],
                                pv[HALF * clip:HALF * (clip + 1), :, par, :], ACT.Copy)
                    last.then_inc(v_ok, 1)
                if runs(n, 1):
                    wait(act, q_sum, n - 1, 1)
                    wait(act, v_sum, n - 1)
                    nc.scalar.activation(latT[:, :], ps_lat, ACT.Copy).then_inc(lat_ok, 1)
                    wait(act, sc_sum, n - 1)
                    for odd in range(2):
                        for clip in range(2):
                            last = nc.scalar.activation(
                                q_bd[HALF * clip:HALF * (clip + 1), odd::2, HALF * clip:HALF * (clip + 1)],
                                ps_q[HALF * odd:HALF * (odd + 1), :, HALF * clip:HALF * (clip + 1)], ACT.Copy)
                    last.then_inc(q_ok, 1)
                if runs(n, 0):
                    wait(act, hid_turned, n, 1)
                    wait(act, y_sum, n)
                    nc.scalar.activation(hidT_hi[:, :, :], ps_xT, ACT.Copy).then_inc(hidT_hi_ok, 1)
                if runs(n, 3):
                    wait(act, o_turned, n - 3, 1)
                    wait(act, at_sum, n - 3)
                    nc.scalar.activation(oT[:, :, :].rearrange("p k c -> p (k c)"), ps_oT, ACT.Copy).then_inc(oT_ok, 1)
                if runs(n, 1):
                    wait(act, k_sum, n - 1, 1)
                    wait(act, k_exp_ok, n - 1)
                    for odd in range(2):
                        for clip in range(2):
                            last = nc.scalar.activation(
                                k_cp[HALF * clip:HALF * (clip + 1), odd::2, :],
                                ps_k[HALF * odd:HALF * (odd + 1), :, HALF * clip:HALF * clip + S], ACT.Copy)
                    last.then_inc(k_cp_ok, 1)
                if runs(n, 2):
                    wait(act, sc_shifted, n - 2, 1)
                    wait(act, p_turned, n - 2)
                    wait(act, sum_ok, n - 2)
                    nc.scalar.activation(probs[:, :, 0:S], shifted[:, :, :], ACT.Exp).then_inc(probs_ok, 1)
                if isinstance(n, int) and n < 2:
                    act.wait_ge(ld_we0, 16 * (n + 1))
                    nc.scalar.activation(we_hi[0][:, n * WCOLS:(n + 1) * WCOLS], we_raw0, ACT.Copy).then_inc(we0_hi, 1)

            steps(act, step)
            act.wait_ge(logit_ok, TILES)
            nc.scalar.activation(u_exp[:, :], logit[:, :], ACT.Exp, bias=neg_bu[:, 0:1], scale=-1.0).then_inc(g_exp, 1)
            act.wait_ge(w_ok, 1)
            act.wait_ge(at_sum, TILES)
            act.wait_ge(xn2_turned, TILES)
            act.wait_ge(y_pad, 1)

            def chunk(e, c):
                g = c + CHUNKS * e
                for f in range(KT):
                    act.wait_ge(f1_sum, g * KT + (f + 1))
                    if f >= 2 or not isinstance(g, int) or g > 0:
                        act.wait_ge(h_lo_ok, g * KT + (f - 1))
                    nc.scalar.activation(h_full[:, f % 2, :], psum[:, bk_f1 + f % 3, 0:CW], ACT.Relu,
                                         bias=b12T[:, e * KT + f:e * KT + f + 1]).then_inc(h_ok, 1)
                    act.wait_ge(h_ok, g * KT + (f + 1))
                    if f >= 4 or not isinstance(g, int) or g > 0:
                        act.wait_ge(f2_sum, g * KT + (f - 3))
                    nc.scalar.activation(h_hi[:, f % 4, :], h_full[:, f % 2, :], ACT.Copy).then_inc(h_hi_ok, 1)
                act.wait_ge(f2_sum, g * KT + KT)
                if not isinstance(g, int) or g > 0:
                    act.wait_ge(ye_turned, g)
                for d in range(KD):
                    col = EXPERTS * KT + e * KD + d
                    nc.scalar.activation(y_sb[:, d, :, 0:S],
                                         psum[:, bk_y + d, 0:CW].rearrange("p (b t) -> p b t", t=S), ACT.Identity,
                                         bias=b12T[:, col:col + 1]).then_inc(ye_ok, 1)
                if e + 1 < EXPERTS:
                    part = bass.ds(PREP * c, PREP)
                    act.wait_ge(ld_we, 32 * (e + 1))
                    if e:
                        act.wait_ge(f2_sum, KT * CHUNKS * e)
                    nc.scalar.activation(we_hi[(e + 1) % 2][:, part], we_raw[:, part], ACT.Copy).then_inc(we_hi_ok, 1)

            chunks(act, chunk)

        @block.vector
        def _(dve):
            for k in range(N_SPLIT):
                dve.wait_ge(setup_hi, k + 1)
                if k < KF:
                    dst, hi = wdT_lo[:, k, :], wdT_hi[:, k, :]
                else:
                    two = slice(2 * (k - KF), 2 * (k - KF) + 2)
                    dst = wpT_lo[:, two, :].rearrange("p a d -> p (a d)")
                    hi = wpT_hi[:, two, :].rearrange("p a d -> p (a d)")
                nc.vector.tensor_tensor(dst, psum[:, k, :], hi.bitcast(F32), ALU.subtract).then_inc(setup_lo, 1)
            dve.wait_ge(ld_att, 5 * 16)
            nc.vector.tensor_tensor(wkv[:, :, :].rearrange("p a b -> p (a b)"), wk_raw, wv_raw, ALU.add).then_inc(wkv_sum, 1)
            dve.wait_ge(zeroed, 8)
            dve.wait_ge(ld_bias, 64)
            hi32 = bias2[32:33, :]
            bias_lo = shifted[:, :, :].rearrange("p h k -> p (h k)")[32:33, 0:F2D + D]
            nc.vector.tensor_copy(hi32, bias_raw[32:33, :]).then_inc(bias_done, 1)
            dve.wait_ge(bias_done, 1)
            nc.vector.tensor_tensor(bias_lo, bias_raw[32:33, :], hi32.bitcast(F32), ALU.subtract).then_inc(bias_done, 1)
            dve.wait_ge(bias_done, 2)
            nc.vector.tensor_copy(hi32, bias_lo).then_inc(bias_done, 1)
            dve.wait_ge(ld_small, 8 * 16)
            nc.vector.tensor_scalar(neg_bu[:, :], neg_bu[:, :], -1.0, None, ALU.mult).then_inc(g_step, 1)

            def step(n):
                if runs(n, 4):
                    wait(dve, at_sum, n - 4, 1)
                    nc.vector.tensor_tensor(tile_rows(n - 4), ps_at, tile_rows(n - 4), ALU.add).then_inc(h1_ok, 1)
                if runs(n, 1):
                    wait(dve, y_rstd_ok, n - 1, 1)
                    if isinstance(n, int) and n == 1:
                        dve.wait_ge(setup_hi, N_SPLIT + 3)
                        dve.wait_ge(setup_pe, N_SPLIT + 2)
                    nc.vector.tensor_scalar(tile_rows(n - 1), ps_y, y_mv[:, 0:1], y_rstd[:, 0:1],
                                            ALU.subtract, ALU.mult).then_inc(y_normed, 1)
                if runs(n, 4):
                    wait(dve, h1_ok, n - 4, 1)
                if runs(n, 0):
                    wait(dve, xT_hi_ok, n, 1)
                    nc.vector.tensor_tensor(xT_lo[:, :, :], ps_xT, xT_hi[:, :, :].bitcast(F32), ALU.subtract).then_inc(xT_lo_ok, 1)
                if runs(n, 4):
                    nc.vector.bn_stats(h1_stats[:, :], tile_rows(n - 4)).then_inc(h1_st_ok, 1)
                    wait(dve, h1_st_ok, n - 4, 1)
                if runs(n, 2):
                    wait(dve, sc_sum, n - 2, 1)
                    nc.vector.tensor_scalar(ps_sc, ps_sc, -CLAMP * SCALE_INV, CLAMP * SCALE_INV,
                                            ALU.max, ALU.min).then_inc(sc_clipped, 1)
                if runs(n, 4):
                    nc.vector.bn_aggr(h1_mv[:, :], h1_stats[:, :]).then_inc(h1_mv_ok, 1)
                if runs(n, 1):
                    wait(dve, h0_ok, n - 1, 1)
                if runs(n, 2):
                    wait(dve, sc_clipped, n - 2, 1)
                    nc.vector.tensor_tensor(ps_sc_h, ps_sc_h,
                                            decay[:, :].unsqueeze(1).unsqueeze(1).broadcast_to([P, 2, 2 * HPQ, S]),
                                            ALU.mult).then_inc(sc_decayed, 1)
                if runs(n, 1):
                    nc.vector.bn_stats(h0_stats[:, :], tile_rows(n - 1)).then_inc(h0_st_ok, 1)
                    wait(dve, h0_st_ok, n - 1, 1)
                if runs(n, 4):
                    wait(dve, h1_rstd_ok, n - 4, 1)
                    wait(dve, xn2_turned, n - 4)
                    nc.vector.tensor_scalar(xn2[:, :], tile_rows(n - 4), h1_mv[:, 0:1], h1_rstd[:, 0:1],
                                            ALU.subtract, ALU.mult).then_inc(xn2_ok, 1)
                if runs(n, 1):
                    nc.vector.bn_aggr(h0_mv[:, :], h0_stats[:, :]).then_inc(h0_mv_ok, 1)
                if runs(n, 4):
                    wait(dve, xn2_ok, n - 4, 1)
                    nc.vector.tensor_tensor_reduce(logit_terms[:, :], xn2[:, :], wu_b[:, :], 1.0, 0.0, ALU.mult, ALU.add,
                                                   logit_one[:, :]).then_inc(logit_one_ok, 1)
                if runs(n, 1):
                    wait(dve, h0_rstd_ok, n - 1, 1)
                    wait(dve, xn_turned, n - 1)
                    nc.vector.tensor_scalar(xn[:, :], tile_rows(n - 1), h0_mv[:, 0:1], h0_rstd[:, 0:1],
                                            ALU.subtract, ALU.mult).then_inc(xn_ok, 1)
                if runs(n, 4):
                    wait(dve, logit_one_ok, n - 4, 1)
                    nc.vector.tensor_scalar(logit[:, bass.ds(n - 4, 1)], logit_one[:, :], 0.0, None, ALU.add).then_inc(logit_ok, 1)
                if runs(n, 2):
                    wait(dve, sc_decayed, n - 2, 1)
                    nc.vector.tensor_reduce(row_max[:, :].rearrange("p (b h) -> p b h", b=2), ps_sc_h, AX.X, ALU.max).then_inc(max_ok, 1)
                    wait(dve, max_ok, n - 2, 1)
                    wait(dve, probs_ok, n - 2)
                    nc.vector.tensor_tensor(
                        shifted[:, :, :].rearrange("p (b h) k -> p b h k", b=2), ps_sc_h,
                        row_max[:, :].rearrange("p (b h) -> p b h", b=2).unsqueeze(3).broadcast_to([P, 2, 2 * HPQ, S]),
                        ALU.subtract).then_inc(sc_shifted, 1)
                if runs(n, 4):
                    wait(dve, x2_hi_ok, n - 4, 1)
                    cols = bass.ds(ROWS * (n - 4), ROWS)
                    nc.vector.tensor_tensor(
                        x2_lo[:, :, cols].rearrange("p k (b t) -> p k b t", b=2),
                        ps_x2T.rearrange("p (k b t) -> p k b t", k=KD, b=2)[:, :, :, 0:S],
                        x2_hi[:, :, cols].rearrange("p k (b t) -> p k b t", b=2).bitcast(F32),
                        ALU.subtract).then_inc(x2_lo_ok, 1)
                if runs(n, 3):
                    wait(dve, pv_sum, n - 3, 1)
                    wait(dve, inv_ok, n - 3, 1)
                    wait(dve, o_turned, n - 3)
                    for clip in range(2):
                        rows = slice(HALF * clip, HALF * (clip + 1))
                        last = nc.vector.tensor_tensor(
                            o_sb[rows, :, :].rearrange("p (h e) d -> p h e d", e=2), ps_pv[rows, :, clip, :, :],
                            row_inv[rows, :].rearrange("p (h e) -> p h e", e=2).unsqueeze(3).broadcast_to([HALF, HEADS // 2, 2, DH]),
                            ALU.mult)
                    last.then_inc(o_ok, 1)
                if runs(n, 0):
                    wait(dve, hidT_hi_ok, n, 1)
                    nc.vector.tensor_tensor(hidT_lo[:, :, :], ps_xT, hidT_hi[:, :, :].bitcast(F32), ALU.subtract).then_inc(hidT_lo_ok, 1)
                if runs(n, 2):
                    wait(dve, probs_ok, n - 2, 1)
                    nc.vector.tensor_reduce(row_sum[:, :], probs[:, :, 0:S], AX.X, ALU.add).then_inc(sum_ok, 1)
                if runs(n, 0):
                    wait(dve, y_sum, n, 1)
                    nc.vector.bn_stats(y_stats[:, :], ps_y).then_inc(y_st_ok, 1)
                    wait(dve, y_st_ok, n, 1)
                if runs(n, 2):
                    wait(dve, sum_ok, n - 2, 1)
                    nc.vector.reciprocal(row_inv[:, :], row_sum[:, :]).then_inc(inv_ok, 1)
                if runs(n, 0):
                    nc.vector.bn_aggr(y_mv[:, :], y_stats[:, :]).then_inc(y_mv_ok, 1)

            steps(dve, step)
            dve.wait_ge(g_exp, 1)
            nc.vector.tensor_scalar(u_den[:, :], u_exp[:, :], 1.0, None, ALU.add).then_inc(g_step, 1)
            dve.wait_ge(g_step, 2)
            nc.vector.reciprocal(u[:, :], u_den[:, :]).then_inc(g_step, 1)
            dve.wait_ge(g_step, 3)
            for e in range(EXPERTS):
                last = nc.vector.tensor_scalar(w_step[:, e, :], u[:, :], gate[:, e:e + 1],
                                               gate[:, EXPERTS + e:EXPERTS + e + 1], ALU.is_gt, ALU.mult)
            last.then_inc(g_step, 1)
            dve.wait_ge(g_step, 4)
            nc.vector.tensor_tensor(w_gate[:, :, :], w_step[:, :, :],
                                    u[:, :].unsqueeze(1).broadcast_to([P, EXPERTS, TILES]), ALU.mult).then_inc(w_ok, 1)
            dve.wait_ge(at_sum, TILES)
            dve.wait_ge(oT_ok, TILES)
            dve.wait_ge(xn2_turned, TILES)

            def add_chunk(e, before, g):
                dve.wait_ge(ye_turned, g)
                flat = w_gate[:, :, :].rearrange("p e t -> p (e t)")
                for j in range(TPC):
                    h = tile_rows(TPC * before + j)
                    last = nc.vector.scalar_tensor_tensor(
                        out=h, in0=ps_yT[:, j, :], scalar=flat[:, bass.ds(TPC * g + (j - TPC), 1)], in1=h,
                        op0=ALU.mult, op1=ALU.add)
                last.then_inc(acc_ok, 1)

            dve.wait_ge(w_ok, 1)
            nc.vector.memset(logit_one[:, :], 0.0).then_inc(acc_ok, 1)

            def chunk(e, c):
                g = c + CHUNKS * e
                for f in range(KT):
                    dve.wait_ge(h_hi_ok, g * KT + (f + 1))
                    nc.vector.tensor_tensor(h_lo[:, f % 4, :], h_full[:, f % 2, :], h_hi[:, f % 4, :].bitcast(F32),
                                            ALU.subtract).then_inc(h_lo_ok, 1)
                    if f == 2 and (not isinstance(g, int) or g > 0):
                        before = (c + (CHUNKS - 1)) % CHUNKS
                        add_chunk(e, before, g)

            chunks(dve, chunk)
            add_chunk(EXPERTS - 1, CHUNKS - 1, CHUNKS * EXPERTS)

        @block.tensor
        def _(pe):
            pe.wait_ge(ld_tok, 3 * 16)
            pe.wait_ge(ld_small, 8 * 16)
            for k in range(KF):
                for g in range(KF):
                    last = nc.tensor.transpose(psum[:, k, g * P:(g + 1) * P], wd_raw[:, g, k * P:(k + 1) * P], ident[:, :])
                last.then_inc(setup_pe, 1)
            for k2 in range(KF // 2):
                for i in range(2):
                    for d in range(KD):
                        k = 2 * k2 + i
                        last = nc.tensor.transpose(psum[:, KF + k2, (KD * i + d) * P:(KD * i + d + 1) * P],
                                                   wp_raw[:, d, k * P:(k + 1) * P], ident[:, :])
                last.then_inc(setup_pe, 1)
            pe.wait_ge(wkv_sum, 1)
            pe.wait_ge(ld_b12, 32)
            for j in range(KD):
                for i in range(KD):
                    nc.tensor.transpose(psum[:, 6, (KD * j + i) * P:(KD * j + i + 1) * P], wkv[:, i, j * P:(j + 1) * P], ident[:, :])
            nb = EXPERTS * (KT + KD)
            nc.tensor.transpose(psum[:, 7, 0:nb], b12_raw[0:nb, :], ident[0:nb, 0:nb]).then_inc(setup_pe, 1)
            pe.wait_ge(setup_hi, N_SPLIT + 2)
            for i in range(KD):
                for j in range(KD):
                    last = nc.tensor.matmul(psum[:, 7, 128 + i * LAT:128 + (i + 1) * LAT], wkvT[:, j, i * P:(i + 1) * P],
                                            wdown[:, j, :], start=(j == 0), stop=(j == KD - 1))
            last.then_inc(setup_pe, 1)
            pe.wait_ge(setup_lo, N_SPLIT)
            pe.wait_ge(setup_hi, N_SPLIT + 3)
            pe.wait_ge(bias_h, 1)
            pe.wait_ge(bias_done, 3)
            pe.wait_ge(ld_up, 32)

            def split_product(dst, lhs_hi, lhs_lo, rhs_hi, rhs_lo, first, last):
                nc.tensor.matmul(dst, lhs_hi, rhs_hi, start=first, stop=False)
                nc.tensor.matmul(dst, lhs_hi, rhs_lo, start=False, stop=False)
                return nc.tensor.matmul(dst, lhs_lo, rhs_hi, start=False, stop=last)

            def step(n):
                if runs(n, 0):
                    wait(pe, x_loaded, n, 1, 64)
                    wait(pe, hidT_lo_ok, n)
                    for k in range(KF):
                        last = nc.tensor.transpose(ps_xT[:, k, :], x_sb[:, k * P:(k + 1) * P], ident[:, :])
                    last.then_inc(x_turned, 1)
                if runs(n, 2):
                    wait(pe, q_ok, n - 2, 1)
                    wait(pe, k_exp_ok, n - 2, 1)
                    wait(pe, sc_shifted, n - 2)
                    for c in range(QUADS):
                        last = nc.tensor.matmul(ps_sc[:, c // 2, (c % 2) * HPQ * S:(c % 2 + 1) * HPQ * S], q_bd[:, c, :],
                                                k_exp[:, c, :, :].rearrange("p h k -> p (h k)"), start=True, stop=True)
                    last.then_inc(sc_sum, 1)
                if runs(n, 3):
                    wait(pe, probs_ok, n - 3, 1)
                    wait(pe, h1_ok, n - 3)
                    for h in range(HEADS // 2):
                        last = nc.tensor.transpose(ps_pT[:, h // 4, (h % 4) * P:(h % 4 + 1) * P],
                                                   probs[:, 2 * h:2 * h + 2, :].rearrange("p e k -> p (e k)"), ident[:, :])
                    last.then_inc(p_turned, 1)
                if runs(n, 0):
                    wait(pe, xT_lo_ok, n, 1)
                    wait(pe, y_normed, n)
                    nc.tensor.matmul(ps_h, ones[:, :], bias2[:, 0:F2D], start=True, stop=False)
                    for k in range(KF):
                        last = split_product(ps_h, xT_hi[:, k, :], xT_lo[:, k, :], wdT_hi[:, k, :], wdT_lo[:, k, :],
                                             False, k == KF - 1)
                    last.then_inc(hid_sum, 1)
                if runs(n, 4):
                    wait(pe, xn2_ok, n - 4, 1)
                    wait(pe, pT_ok, n - 4, 2)
                    for k in range(KD):
                        last = nc.tensor.transpose(ps_x2T[:, k * P:(k + 1) * P], xn2[:, k * P:(k + 1) * P], ident[:, :])
                    last.then_inc(xn2_turned, 1)
                if runs(n, 3):
                    wait(pe, pT_ok, n - 3, 1)
                    wait(pe, v_ok, n - 3, 1)
                    wait(pe, k_cp_ok, n - 3, 2)
                    for h in range(HEADS // 2):
                        last = nc.tensor.matmul(ps_pv[:, h, :, :, :].rearrange("p b e d -> p (b e d)"), pT[:, h, :],
                                                v_bd[:, h, :, :, :].rearrange("p b e d -> p (b e d)"), start=True, stop=True)
                    last.then_inc(pv_sum, 1)
                if runs(n, 1):
                    wait(pe, xn_ok, n - 1, 1)
                    wait(pe, q_ok, n - 1)
                    for k in range(KD):
                        last = nc.tensor.transpose(ps_xnT[:, k * P:(k + 1) * P], xn[:, k * P:(k + 1) * P], ident[:, :])
                    last.then_inc(xn_turned, 1)
                if runs(n, 0):
                    wait(pe, hid_ok, n, 1)
                    for k in range(KF):
                        last = nc.tensor.transpose(ps_xT[:, k, :], hid[:, k * P:(k + 1) * P], ident[:, :])
                    last.then_inc(hid_turned, 1)
                if runs(n, 2):
                    wait(pe, lat_ok, n - 2, 1)
                    if runs(n, 3):
                        wait(pe, pT_ok, n - 3, 1)
                    nc.tensor.matmul(ps_v, latT[:, :], wup[:, D:], start=True, stop=True).then_inc(v_sum, 1)
                if runs(n, 1):
                    wait(pe, xnT_ok, n - 1, 1)
                    for k in range(KD):
                        nc.tensor.matmul(ps_lat, wkvd[:, k, :], xnT[:, k, :], start=(k == 0), stop=(k == KD - 1))
                    for m in range(KD):
                        for k in range(KD):
                            last = nc.tensor.matmul(ps_q[:, m, :], wq[:, k, m * P:(m + 1) * P], xnT[:, k, :],
                                                    start=(k == 0), stop=(k == KD - 1))
                    last.then_inc(q_sum, 1)
                if runs(n, 3):
                    wait(pe, o_ok, n - 3, 1)
                    if runs(n, 4):
                        wait(pe, x2_lo_ok, n - 4, 1)
                    for k in range(KD):
                        last = nc.tensor.transpose(ps_oT[:, k * P:(k + 1) * P],
                                                   o_sb[:, k * P // DH:(k + 1) * P // DH, :].rearrange("p h d -> p (h d)"), ident[:, :])
                    last.then_inc(o_turned, 1)
                if runs(n, 1):
                    wait(pe, lat_ok, n - 1, 1)
                    wait(pe, o_ok, n - 1, -1)
                    for m in range(KD):
                        last = nc.tensor.matmul(ps_k[:, m, :], wup[:, m * P:(m + 1) * P], latT[:, :], start=True, stop=True)
                    last.then_inc(k_sum, 1)
                if runs(n, 0):
                    wait(pe, hidT_lo_ok, n, 1)
                    nc.tensor.matmul(ps_y, ones[:, :], bias2[:, F2D:], start=True, stop=False)
                    for k in range(KF):
                        last = split_product(ps_y, hidT_hi[:, k, :], hidT_lo[:, k, :], wpT_hi[:, k, :], wpT_lo[:, k, :],
                                             False, k == KF - 1)
                    last.then_inc(y_sum, 1)
                if runs(n, 3):
                    wait(pe, oT_ok, n - 3, 1)
                    wait(pe, v_ok, n - 3, 2)
                    for k in range(KD):
                        last = nc.tensor.matmul(ps_at, oT[:, k, :], wo[:, k, :], start=(k == 0), stop=(k == KD - 1))
                    last.then_inc(at_sum, 1)

            steps(pe, step)
            pe.wait_ge(h1_ok, TILES)
            pe.wait_ge(x2_lo_ok, TILES)
            pe.wait_ge(we0_lo, 2)

            def first_layer(e, g, c, f):
                if f >= 3:
                    pe.wait_ge(h_ok, g * KT + (f - 2))
                elif not isinstance(g, int) or g > 0:
                    pe.wait_ge(h_ok, g * KT - (1, 0, 2)[f])
                w_hi = we_hi[e % 2][:, 0:WCOLS].rearrange("p (k f) -> p k f", k=KD)
                w_lo = we_lo[e % 2][:, 0:WCOLS].rearrange("p (k f) -> p k f", k=KD)
                cols, feats = bass.ds(CW * c, CW), slice(f * P, (f + 1) * P)
                for k in range(KD):
                    last = split_product(psum[:, bk_f1 + f % 3, 0:CW], w_hi[:, k, feats], w_lo[:, k, feats],
                                         x2_hi[:, k, cols], x2_lo[:, k, cols], k == 0, k == KD - 1)
                last.then_inc(f1_sum, 1)

            def second_layer(e, g, f):
                pe.wait_ge(h_lo_ok, g * KT + (f + 1))
                if f == 0 and (not isinstance(g, int) or g > 0):
                    pe.wait_ge(ye_ok, g * KD)
                w_hi = we_hi[e % 2][:, WCOLS:].rearrange("p (k d) -> p k d", k=KT)
                w_lo = we_lo[e % 2][:, WCOLS:].rearrange("p (k d) -> p k d", k=KT)
                for d in range(KD):
                    last = split_product(psum[:, bk_y + d, 0:CW], w_hi[:, f, d * P:(d + 1) * P], w_lo[:, f, d * P:(d + 1) * P],
                                         h_hi[:, f % 4, :], h_lo[:, f % 4, :], f == 0, f == KT - 1)
                last.then_inc(f2_sum, 1)

            def turn_chunk(g):
                pe.wait_ge(ye_ok, g * KD)
                pe.wait_ge(acc_ok, g)
                for j in range(TPC):
                    for d in range(KD):
                        last = nc.tensor.transpose(ps_yT[:, j, d * P:(d + 1) * P],
                                                   y_sb[:, d, 2 * j:2 * j + 2, :].rearrange("p b t -> p (b t)"), ident[:, :])
                last.then_inc(ye_turned, 1)

            def chunk(e, c):
                g = c + CHUNKS * e
                if e and not isinstance(c, int):
                    pe.wait_ge(we_lo_ok, CHUNKS * e)
                for f in range(3):
                    first_layer(e, g, c, f)
                if not isinstance(g, int) or g > 0:
                    turn_chunk(g)
                for f in range(KT):
                    second_layer(e, g, f)
                    if f + 3 < KT:
                        first_layer(e, g, c, f + 3)

            chunks(pe, chunk)
            turn_chunk(CHUNKS * EXPERTS)


_INS = ['x', 'L0_tok_Wd', 'L0_tok_bd', 'L0_tok_Wp', 'L0_tok_bp', 'L0_tok_gamma', 'L0_tok_beta', 'L0_attn_Wq',
        'L0_attn_Wk', 'L0_attn_Wv', 'L0_attn_Wo', 'L0_attn_W_down_kv', 'L0_attn_W_up_k', 'L0_attn_W_up_v',
        'L0_ffn_W1', 'L0_ffn_b1', 'L0_ffn_W2', 'L0_ffn_b2', 'L0_ffn_Wu', 'L0_ffn_bu']
_OUT = (CLIPS, S, D)


def constants():
    import numpy as np
    row = np.arange(P) % HALF
    decay = np.exp(np.float32(-0.01 * 0.01) * np.abs(row[:, None] - np.arange(S)[None, :]).astype(np.float32))
    headmask = (row[:, None] // DH == np.arange(HPQ)[None, :]).astype(np.float32)
    step = (np.arange(EXPERTS)[None, :] - row[:, None]) % EXPERTS + 1
    gate = np.concatenate([np.where(step == 1, -1.0, (step - 1) / EXPERTS), 1.0 / step], axis=1)
    return {"c_ident": np.eye(P, dtype=np.float32), "c_decay": (decay / np.float32(SCALE_INV)).astype(np.float32),
            "c_headmask": headmask, "c_gate": gate.astype(np.float32)}


def kernel(**inputs):
    import numpy as _np
    import concourse.bacc as _bacc
    from concourse import mybir as _mybir
    from concourse.bass_utils import run_bass_kernel_spmd as _run

    nc = _bacc.Bacc("TRN2", target_bir_lowering=False, num_devices=1)
    arrays, args = {}, []
    tables = constants()
    for name in _INS + list(tables):
        a = _np.ascontiguousarray(tables[name] if name in tables else inputs[name])
        arrays[f"in_{name}_dram"] = a
        args.append(nc.dram_tensor(f"in_{name}_dram", a.shape, _mybir.dt.from_np(a.dtype), kind="ExternalInput").ap())
    args.append(nc.dram_tensor("out_0_dram", _OUT, F32, kind="ExternalOutput").ap())
    build(nc, *args)
    r = _run(nc, [arrays], core_ids=[0])
    return r.results[0]["out_0_dram"]
```

```python
from contextlib import ExitStack

import concourse.bass as bass
from concourse import mybir

F32 = mybir.dt.float32
F32R = mybir.dt.float32r
ALU = mybir.AluOpType
ACT = mybir.ActivationFunctionType
AX = mybir.AxisListType

P = 128
CLIPS, FRAMES, D = 64, 125, 256
S = FRAMES // 2
HALF = 64
TILES = CLIPS // 2
ROWS = 2 * S
F2D = 2 * D
HEADS, DH, LAT = 16, 16, 64
QUADS, HPQ = 4, 4
FF, EXPERTS = 1024, 4
KD, KF, KT = D // P, F2D // P, FF // P
CHUNKS, TPC = 8, TILES // 8
CW = TPC * ROWS
LN_EPS = 1e-5
CLAMP = 10000.0
SCALE_INV = 16.0
LAST_LAG = 4
PEELED = 3
WCOLS = KD * FF
PREP = 2 * WCOLS // CHUNKS


def build(nc, x, Wd, bd, Wp, bp, gamma, beta, Wq, Wk, Wv, Wo, Wdown, Wupk, Wupv,
          W1, b1, W2, b2, Wu, bu, c_ident, c_decay, c_headmask, c_gate, out):
    ctx = ExitStack()
    with ctx:
        def sem(name):
            return ctx.enter_context(nc.semaphore(name))

        def sb(name, shape, dt=F32, stack=None):
            return (stack or ctx).enter_context(nc.sbuf_tensor(name, shape, dt))

        x2_hi = sb("x2_hi", [P, KD, TILES * ROWS], F32R)
        x2_lo = sb("x2_lo", [P, KD, TILES * ROWS], F32R)
        resid = sb("resid", [P, TILES, D])
        we_hi = [sb("we_hi0", [P, 2 * WCOLS], F32R)]
        we_lo = [sb("we_lo0", [P, 2 * WCOLS], F32R)]
        ident = sb("ident_sb", [P, P])
        b1T = sb("b1T", [P, EXPERTS * KT])
        b2_b = sb("b2_b", [P, EXPERTS, D])
        gate = sb("gate", [P, 2 * EXPERTS])
        logit = sb("logit", [P, TPC])
        u_exp = sb("u_exp", [P, TPC])
        u_den = sb("u_den", [P, TPC])
        u = sb("u", [P, TPC])
        w_step = sb("w_step", [P, EXPERTS, TPC])
        neg_bu = sb("neg_bu", [P, 1])
        eps = sb("eps", [P, 1])
        tick = sb("tick", [P, 1])
        w_gate = sb("w_gate", [P, EXPERTS, TILES])
        psum = ctx.enter_context(nc.psum_tensor("psum", [P, 8, 512], F32))

        scratch = resid[:, :, :].rearrange("p t d -> p (t d)")
        used = [0]

        def stage(cols):
            used[0] += cols
            return scratch[:, used[0] - cols:used[0]]

        wd_raw = stage(KF * F2D).rearrange("p (a b) -> p a b", a=KF)
        wp_raw = stage(KD * F2D).rearrange("p (a b) -> p a b", a=KD)
        wk_raw = stage(KD * D)
        wv_raw = stage(KD * D)
        wkv = stage(KD * D).rearrange("p (a b) -> p a b", a=KD)
        wkvT = stage(KD * D).rearrange("p (a b) -> p a b", a=KD)
        wdown = stage(KD * LAT).rearrange("p (a b) -> p a b", a=KD)
        b1_raw = stage(P)
        we_raw0 = stage(WCOLS)
        bias_raw = stage(F2D + D)
        assert used[0] <= TILES * D

        pa = ExitStack()
        wdT_hi = sb("wdT_hi", [P, KF, F2D], F32R, pa)
        wdT_lo = sb("wdT_lo", [P, KF, F2D], F32R, pa)
        wpT_hi = sb("wpT_hi", [P, KF, D], F32R, pa)
        wpT_lo = sb("wpT_lo", [P, KF, D], F32R, pa)
        wq = sb("wq", [P, KD, D], stack=pa)
        wo = sb("wo", [P, KD, D], stack=pa)
        wkvd = sb("wkvd", [P, KD, LAT], stack=pa)
        wup = sb("wup", [LAT, 2 * D], stack=pa)
        bias2 = sb("bias2", [P, F2D + D], F32R, pa)
        ones = sb("ones", [P, P], F32R, pa)
        gamma_b = sb("gamma_b", [P, D], stack=pa)
        beta_b = sb("beta_b", [P, D], stack=pa)
        wu_b = sb("wu_b", [P, D], stack=pa)
        decay = sb("decay", [P, S], stack=pa)
        headmask = sb("headmask", [P, HPQ], stack=pa)
        neg_half = sb("neg_half", [P, 1], stack=pa)
        x_sb = sb("x_sb", [P, F2D], stack=pa)
        xT_hi = sb("xT_hi", [P, KF, P], F32R, pa)
        xT_lo = sb("xT_lo", [P, KF, P], F32R, pa)
        ha_hi = sb("ha_hi", [P, 2 * TPC, HALF], F32R, pa)
        ha_lo = sb("ha_lo", [P, 2 * TPC, HALF], F32R, pa)
        hid = sb("hid", [P, F2D], stack=pa)
        y_stats = sb("y_stats", [P, 6], stack=pa)
        y_mv = sb("y_mv", [P, 2], stack=pa)
        y_ve = sb("y_ve", [P, 1], stack=pa)
        y_rstd = sb("y_rstd", [P, 1], stack=pa)
        h0_stats = sb("h0_stats", [P, 6], stack=pa)
        h0_mv = sb("h0_mv", [P, 2], stack=pa)
        h0_ve = sb("h0_ve", [P, 1], stack=pa)
        h0_rstd = sb("h0_rstd", [P, 1], stack=pa)
        h1_stats = sb("h1_stats", [P, 6], stack=pa)
        h1_mv = sb("h1_mv", [P, 2], stack=pa)
        h1_ve = sb("h1_ve", [P, 1], stack=pa)
        h1_rstd = sb("h1_rstd", [P, 1], stack=pa)
        xn = sb("xn", [P, D], stack=pa)
        xnT = sb("xnT", [P, KD, P], stack=pa)
        latT = sb("latT", [LAT, P], stack=pa)
        q_bd = sb("q_bd", [P, QUADS, P], stack=pa)
        k_cp = sb("k_cp", [P, QUADS, S], stack=pa)
        k_exp = sb("k_exp", [P, QUADS, HPQ, S], stack=pa)
        v_bd = sb("v_bd", [P, HEADS // 2, 2, 2, DH], stack=pa)
        row_max = sb("row_max", [P, HEADS], stack=pa)
        row_sum = sb("row_sum", [P, HEADS], stack=pa)
        row_inv = sb("row_inv", [P, HEADS], stack=pa)
        probs = sb("probs", [P, HEADS, HALF], stack=pa)
        pT = sb("pT", [P, HEADS // 2, P], stack=pa)
        o_sb = sb("o_sb", [P, HEADS, DH], stack=pa)
        oT = sb("oT", [P, KD, P], stack=pa)
        xn2 = sb("xn2", [P, D], stack=pa)
        logit_terms = sb("logit_terms", [P, D], stack=pa)
        pa.close()

        pb = ExitStack()
        we_raw = sb("we_raw", [P, 2 * WCOLS], stack=pb)
        we_hi.append(sb("we_hi1", [P, 2 * WCOLS], F32R, pb))
        we_lo.append(sb("we_lo1", [P, 2 * WCOLS], F32R, pb))
        h_hi = sb("h_hi", [P, 4, 2 * TPC, HALF], F32R, pb)
        h_lo = sb("h_lo", [P, 4, 2 * TPC, HALF], F32R, pb)
        pb.close()

        bk_f, bk_y, bk_s, bk_h, bk_x, bk_o = (0, 5, 6), 1, 3, 5, 6, 7
        ps_xT = psum[:, bk_x, :].rearrange("p (k c) -> p k c", k=KF)
        ps_x2T = psum[:, bk_x, 0:KD * P]
        ps_xnT = psum[:, bk_x, 0:KD * P]
        ps_q = psum[:, bk_x, 0:KD * P].rearrange("p (m c) -> p m c", m=KD)
        ps_lat = psum[0:LAT, bk_s, 0:P]
        ps_sc = psum[:, bk_s:bk_s + 2, 0:2 * HPQ * S]
        ps_sc_h = ps_sc.rearrange("p b (h k) -> p b h k", k=S)
        ps_pT = psum[:, bk_s:bk_s + 2, :]
        ps_h = psum[:, bk_h, :]
        ps_hT = psum[:, bk_h, :].rearrange("p (k c) -> p k c", k=KF)
        ps_y = psum[:, bk_h, 0:D]
        ps_v = psum[:, bk_s + 1, 0:D]
        ps_at = psum[:, bk_o, 0:D]
        ps_oT = psum[:, bk_o, 0:KD * P]
        ps_k = psum[:, bk_s + 1, 0:KD * P].rearrange("p (m c) -> p m c", m=KD)
        ps_pv = psum[:, bk_o, :].rearrange("p (h b e d) -> p h b e d", h=HEADS // 2, b=2, e=2)
        ps_e = psum[:, bk_y:bk_y + 2, :].rearrange("p b (j d) -> p (b j) d", j=2)

        ld_ident, ld_wd, ld_wp, ld_kv, ld_down = (sem(s) for s in ("ld_ident", "ld_wd", "ld_wp", "ld_kv", "ld_down"))
        ld_att, ld_small, ld_b1, ld_up = (sem(s) for s in ("ld_att", "ld_small", "ld_b1", "ld_up"))
        ld_bias, ld_we0, ld_we = sem("ld_bias"), sem("ld_we0"), sem("ld_we")
        zeroed, wkv_sum, setup_pe, setup_hi, setup_lo = (sem(s) for s in ("zeroed", "wkv_sum", "setup_pe", "setup_hi", "setup_lo"))
        bias_h, bias_done, we0_hi, we0_lo = sem("bias_h"), sem("bias_done"), sem("we0_hi"), sem("we0_lo")
        x_loaded = sem("x_loaded")
        x_turned, xT_hi_ok, xT_lo_ok, hid_sum = sem("x_turned"), sem("xT_hi_ok"), sem("xT_lo_ok"), sem("hid_sum")
        hid_ok, hid_turned, hidT_hi_ok, hidT_lo_ok = sem("hid_ok"), sem("hid_turned"), sem("hidT_hi_ok"), sem("hidT_lo_ok")
        y_sum, y_st_ok, y_mv_ok, y_ve_ok, y_rstd_ok = (sem(s) for s in ("y_sum", "y_st_ok", "y_mv_ok", "y_ve_ok", "y_rstd_ok"))
        y_normed, y_scaled, h0_ok = sem("y_normed"), sem("y_scaled"), sem("h0_ok")
        h0_st_ok, h0_mv_ok, h0_ve_ok, h0_rstd_ok = sem("h0_st_ok"), sem("h0_mv_ok"), sem("h0_ve_ok"), sem("h0_rstd_ok")
        xn_ok, xn_turned, xnT_ok, q_sum = sem("xn_ok"), sem("xn_turned"), sem("xnT_ok"), sem("q_sum")
        lat_ok, q_ok, k_sum, k_cp_ok, k_exp_ok = (sem(s) for s in ("lat_ok", "q_ok", "k_sum", "k_cp_ok", "k_exp_ok"))
        v_sum, v_ok, lat_sum = sem("v_sum"), sem("v_ok"), sem("lat_sum")
        sc_sum, sc_clipped, sc_decayed, max_ok, sc_shifted = (sem(s) for s in ("sc_sum", "sc_clipped", "sc_decayed", "max_ok", "sc_shifted"))
        probs_ok, sum_ok, inv_ok, p_turned, pT_ok = (sem(s) for s in ("probs_ok", "sum_ok", "inv_ok", "p_turned", "pT_ok"))
        pv_sum, o_ok, o_turned, oT_ok, at_sum = (sem(s) for s in ("pv_sum", "o_ok", "o_turned", "oT_ok", "at_sum"))
        h1_ok, h1_st_ok, h1_mv_ok, h1_ve_ok, h1_rstd_ok = (sem(s) for s in ("h1_ok", "h1_st_ok", "h1_mv_ok", "h1_ve_ok", "h1_rstd_ok"))
        xn2_ok, xn2_turned, x2_hi_ok, x2_lo_ok, logit_ok = (sem(s) for s in ("xn2_ok", "xn2_turned", "x2_hi_ok", "x2_lo_ok", "logit_ok"))

        g_exp, g_step, w_ok = sem("g_exp"), sem("g_step"), sem("w_ok")
        f1_sum, h_ok, h_hi_ok, h_lo_ok, f2_sum = (sem(s) for s in ("f1_sum", "h_ok", "h_hi_ok", "h_lo_ok", "f2_sum"))
        h_pad, y_added, b2_added = sem("h_pad"), sem("y_added"), sem("b2_added")
        we_hi_ok, we_lo_ok, stored = sem("we_hi_ok"), sem("we_lo_ok"), sem("stored")

        N_SPLIT = KF + KF // 2
        wp_bank = (4, 7)
        N_SMALL = 8

        def runs(n, lag):
            return not isinstance(n, int) or 0 <= n - lag < TILES

        def wait(eng, s, n, more=0, each=1):
            if isinstance(n, int):
                count = min(n + more, TILES) * each
                if count > 0:
                    eng.wait_ge(s, count)
            else:
                eng.wait_ge(s, (n + more) * each)

        def tile_rows(t):
            return resid[:, bass.ds(t, 1), :].rearrange("p t d -> p (t d)")

        def clips_of(bank):
            return psum[:, bank, 0:CW].rearrange("p (b t) -> p b t", t=S)

        def steps(eng, step):
            for m in range(PEELED):
                for j in range(TPC):
                    step(m, j, TPC * m + j)
            with eng.Fori(PEELED, CHUNKS) as m:
                for j in range(TPC):
                    step(m, j, m * TPC + j)
            for j in range(LAST_LAG):
                step(CHUNKS, j, TILES + j)

        def ffn_in_window(m):
            return not isinstance(m, int) or m >= 2

        PARTS = 2 * TPC

        def parts_in(n):
            return {1: (0, 1), 2: (2, 3), 4: (4,), 5: (5,), 6: (6,), 7: (7,)}.get(n, ()) if isinstance(n, int) else ()

        def part0(n):
            return slice(n * 2 * WCOLS // PARTS, (n + 1) * 2 * WCOLS // PARTS)

        def raw_part(n):
            a = n % (PARTS // 2) * 2 * WCOLS // PARTS
            return we_raw0[:, a:a + 2 * WCOLS // PARTS]

        def drains(m):
            return isinstance(m, int) and m == CHUNKS

        def bank_of(m, f):
            return bk_h if drains(m) and f % 2 else bk_f[0]

        def older(m, age):
            return not isinstance(m, int) or m >= age

        def chunks(eng, chunk):
            chunk(0, CHUNKS - 1)
            for e in range(1, EXPERTS):
                chunk(e, 0)
                with eng.Fori(1, CHUNKS) as c:
                    chunk(e, c)

        block = ctx.enter_context(nc.Block())

        @block.sync
        def _(sp):
            sp.dma_start(ident[:, :], c_ident).then_inc(ld_ident, 16)
            for t in range(2):
                sp.dma_start(wd_raw[:, 2 * t:2 * t + 2, :], Wd.rearrange("(a p) f -> p a f", p=P)[:, 2 * t:2 * t + 2, :]).then_inc(ld_wd, 16)
            sp.dma_start(wp_raw, Wp.rearrange("(a p) f -> p a f", p=P)).then_inc(ld_wp, 16)
            sp.wait_ge(zeroed, 1)

            def load_x(n):
                if not runs(n, 0):
                    return
                wait(sp, x_turned, n)
                for half in range(2):
                    rows = x[bass.ds(2 * n + half, 1), 0:2 * S, :].rearrange("a (t j) d -> (a t) (j d)", j=2)
                    for a, b in ((0, 48), (48, S)):
                        sp.dma_start(x_sb[HALF * half + a:HALF * half + b, :], rows[a:b, :]).then_inc(x_loaded, 16)

            load_x(0)
            for row in (0, 32):
                sp.dma_start(bias_raw[row:row + 1, 0:F2D], bd.rearrange("(a d) -> a d", a=1)).then_inc(ld_bias, 16)
                sp.dma_start(bias_raw[row:row + 1, F2D:], bp.rearrange("(a d) -> a d", a=1)).then_inc(ld_bias, 16)
            sp.dma_start(b1_raw[0:EXPERTS * KT, :], b1.rearrange("e (f p) -> (e f) p", p=P)).then_inc(ld_b1, 16)
            for src, dst, done in ((Wk, wk_raw, ld_kv), (Wv, wv_raw, ld_kv), (Wdown, wdown, ld_down), (Wq, wq, ld_att), (Wo, wo, ld_att)):
                d = dst if len(dst.shape) == 3 else dst.rearrange("p (a b) -> p a b", a=KD)
                sp.dma_start(d[:, :, :], src.rearrange("(a p) f -> p a f", p=P)).then_inc(done, 16)
            sp.dma_start(wup[:, 0:D], Wupk).then_inc(ld_up, 16)
            sp.dma_start(wup[:, D:], Wupv).then_inc(ld_up, 16)
            sp.dma_start(gamma_b[:, :], gamma.partition_broadcast(P)).then_inc(ld_small, 16)
            sp.dma_start(beta_b[:, :], beta.partition_broadcast(P)).then_inc(ld_small, 16)
            sp.dma_start(wu_b[:, :], Wu.rearrange("d o -> (d o)").partition_broadcast(P)).then_inc(ld_small, 16)
            sp.dma_start(neg_bu[:, :], bu.partition_broadcast(P)).then_inc(ld_small, 16)
            sp.dma_start(decay[:, :], c_decay).then_inc(ld_small, 16)
            sp.dma_start(headmask[:, :], c_headmask).then_inc(ld_small, 16)
            sp.dma_start(gate[:, :], c_gate).then_inc(ld_small, 16)
            sp.dma_start(b2_b[:, :, :].rearrange("p e d -> p (e d)"), b2.rearrange("e d -> (e d)").partition_broadcast(P)).then_inc(ld_small, 16)
            sp.dma_start(we_raw0.rearrange("p (k f) -> p k f", k=KD), W1[0].rearrange("(k p) f -> p k f", p=P)).then_inc(ld_we0, 16)

            def step(m, j, n):
                if isinstance(n, int) and n == 0:
                    return
                load_x(n)
                if isinstance(n, int) and n == 3:
                    sp.wait_ge(we0_lo, PARTS // 2)
                    sp.dma_start(we_raw0.rearrange("p (k f) -> p k f", k=KT), W2[0].rearrange("(k p) f -> p k f", p=P)).then_inc(ld_we0, 16)

            steps(sp, step)
            sp.wait_ge(y_sum, TILES)
            for e in range(1, EXPERTS):
                if e > 1:
                    sp.wait_ge(we_lo_ok, CHUNKS * (e - 1))
                sp.dma_start(we_raw[:, 0:WCOLS].rearrange("p (k f) -> p k f", k=KD), W1[e].rearrange("(k p) f -> p k f", p=P)).then_inc(ld_we, 16)
                sp.dma_start(we_raw[:, WCOLS:].rearrange("p (k f) -> p k f", k=KT), W2[e].rearrange("(k p) f -> p k f", p=P)).then_inc(ld_we, 16)
            with sp.Fori(0, CHUNKS) as c:
                sp.wait_ge(y_added, c * TPC + TPC * ((EXPERTS - 1) * CHUNKS + 1))
                sp.wait_ge(b2_added, c * TPC + TPC * ((EXPERTS - 1) * CHUNKS + 1))
                o = out.rearrange("(c j h) t d -> c h t j d", j=TPC, h=2)[bass.ds(c, 1)].rearrange("c h t j d -> (c h) t j d")
                r = resid[:, bass.ds(TPC * c, TPC), :]
                for half in range(2):
                    for a, b in ((0, 48), (48, S)):
                        sp.dma_start(o[half, a:b], r[HALF * half + a:HALF * half + b, :, :]).then_inc(stored, 16)
            sp.wait_ge(stored, 16 * 4 * CHUNKS)

        @block.gpsimd
        def _(pool):
            nc.gpsimd.memset(x_sb[:, :], 0.0).then_inc(zeroed, 1)
            nc.gpsimd.memset(bias2[:, :].bitcast(F32), 0.0).then_inc(zeroed, 1)
            nc.gpsimd.memset(ones[:, :].bitcast(F32), 1.0).then_inc(zeroed, 1)
            nc.gpsimd.memset(neg_half[:, :], -0.5).then_inc(zeroed, 1)
            nc.gpsimd.memset(eps[:, :], LN_EPS).then_inc(zeroed, 1)
            nc.gpsimd.memset(probs[:, :, :], 0.0).then_inc(zeroed, 1)
            nc.gpsimd.memset(q_bd[:, :, :], 0.0).then_inc(zeroed, 1)
            nc.gpsimd.memset(v_bd[:, :, :, :, :], 0.0).then_inc(zeroed, 1)
            for ha in (ha_hi, ha_lo):
                nc.gpsimd.memset(ha[:, :, S:].bitcast(F32), 0.0).then_inc(h_pad, 1)
            pool.wait_ge(ld_bias, 64)
            hi32 = bias2[32:33, :]
            pool.wait_ge(zeroed, 8)
            pool.wait_ge(h_pad, 2)
            nc.gpsimd.tensor_copy(hi32, bias_raw[32:33, :]).then_inc(bias_done, 1)
            pool.wait_ge(bias_done, 1)
            nc.gpsimd.tensor_tensor(hi32, bias_raw[32:33, :], hi32.bitcast(F32), ALU.subtract).then_inc(bias_done, 1)
            pool.wait_ge(bias_done, 2)
            pool.wait_ge(ld_small, N_SMALL * 16)

            def rstd(n, mv, mv_ok, ve, ve_ok, r, r_ok):
                wait(pool, mv_ok, n, 1)
                nc.gpsimd.tensor_tensor(ve[:, :], mv[:, 1:2], eps[:, :], ALU.add).then_inc(ve_ok, 1)
                wait(pool, ve_ok, n, 1)
                nc.gpsimd.tensor_tensor(r[:, :], ve[:, :], neg_half[:, :], ALU.pow).then_inc(r_ok, 1)

            def pause():
                nc.gpsimd.tensor_tensor(tick[:, :], eps[:, :], eps[:, :], ALU.add)

            def step(m, j, n):
                if runs(n, 1):
                    h = tile_rows(n - 1)
                    wait(pool, y_normed, n - 1, 1)
                    pause()
                    nc.gpsimd.tensor_tensor(h, h, gamma_b[:, :], ALU.mult).then_inc(y_scaled, 1)
                    wait(pool, y_scaled, n - 1, 1)
                    pause()
                    nc.gpsimd.tensor_tensor(h, h, beta_b[:, :], ALU.add).then_inc(h0_ok, 1)
                if runs(n, 4):
                    rstd(n - 4, h1_mv, h1_mv_ok, h1_ve, h1_ve_ok, h1_rstd, h1_rstd_ok)
                for i in parts_in(n):
                    pool.wait_ge(we0_hi, i + 1)
                    nc.gpsimd.tensor_tensor(we_lo[0][:, part0(i)], raw_part(i), we_hi[0][:, part0(i)].bitcast(F32),
                                            ALU.subtract).then_inc(we0_lo, 1)
                if runs(n, 1):
                    rstd(n - 1, h0_mv, h0_mv_ok, h0_ve, h0_ve_ok, h0_rstd, h0_rstd_ok)
                if runs(n, 0):
                    rstd(n, y_mv, y_mv_ok, y_ve, y_ve_ok, y_rstd, y_rstd_ok)
                if runs(n, 1):
                    wait(pool, k_cp_ok, n - 1, 1)
                    wait(pool, sc_sum, n - 1)
                    nc.gpsimd.tensor_tensor(
                        k_exp[:, :, :, :],
                        k_cp[:, :, :].unsqueeze(2).broadcast_to([P, QUADS, HPQ, S]),
                        headmask[:, :].unsqueeze(1).unsqueeze(3).broadcast_to([P, QUADS, HPQ, S]),
                        ALU.mult).then_inc(k_exp_ok, 1)

            steps(pool, step)
            pool.wait_ge(at_sum, TILES)
            for h in (h_hi, h_lo):
                nc.gpsimd.memset(h[:, :, :, S:].bitcast(F32), 0.0).then_inc(h_pad, 1)
            for e in range(1, EXPERTS):
                with pool.Fori(0, CHUNKS) as c:
                    part = bass.ds(PREP * c, PREP)
                    pool.wait_ge(we_hi_ok, c + (CHUNKS * (e - 1) + 1))
                    nc.gpsimd.tensor_tensor(we_lo[e % 2][:, part], we_raw[:, part],
                                            we_hi[e % 2][:, part].bitcast(F32), ALU.subtract).then_inc(we_lo_ok, 1)

        @block.scalar
        def _(act):
            for k in range(KF):
                act.wait_ge(setup_pe, k + 1)
                nc.scalar.activation(wdT_hi[:, k, :], psum[:, k, :], ACT.Copy).then_inc(setup_hi, 1)

            def split_wp():
                act.wait_ge(zeroed, 8)
                act.wait_ge(ld_bias, 64)
                nc.scalar.activation(bias2[0:1, :], bias_raw[0:1, :], ACT.Copy).then_inc(bias_h, 1)
                for k in range(KF // 2):
                    act.wait_ge(setup_pe, KF + k + 1)
                    nc.scalar.activation(wpT_hi[:, 2 * k:2 * k + 2, :].rearrange("p a d -> p (a d)"), psum[:, wp_bank[k], :], ACT.Copy).then_inc(setup_hi, 1)

            def copy_wkv():
                act.wait_ge(setup_pe, N_SPLIT + 1)
                nc.scalar.activation(wkvT[:, :, :].rearrange("p a b -> p (a b)"), psum[:, 6, :], ACT.Copy).then_inc(setup_hi, 1)
                nc.scalar.activation(b1T[:, :], psum[:, 7, 0:EXPERTS * KT], ACT.Copy).then_inc(setup_hi, 1)

            def copy_wkvd():
                act.wait_ge(setup_pe, N_SPLIT + 2)
                nc.scalar.activation(wkvd[:, :, :].rearrange("p a b -> p (a b)"), psum[:, 7, 128:128 + KD * LAT], ACT.Copy).then_inc(setup_hi, 1)

            def hidden_relu(e, g, f, bank):
                act.wait_ge(f1_sum, g * KT + (f + 1))
                nc.scalar.activation(psum[:, bank, 0:CW], psum[:, bank, 0:CW], ACT.Relu,
                                     bias=b1T[:, e * KT + f:e * KT + f + 1]).then_inc(h_ok, 1)

            def hidden_hi(g, f, bank, hi, used):
                act.wait_ge(h_ok, g * KT + (f + 1))
                if not isinstance(used, int) or used > 0:
                    act.wait_ge(f2_sum, used)
                nc.scalar.activation(hi[:, :, 0:S], clips_of(bank), ACT.Copy).then_inc(h_hi_ok, 1)

            def gate_exp(c):
                act.wait_ge(logit_ok, c * TPC + TPC)
                nc.scalar.activation(u_exp[:, :], logit[:, :], ACT.Exp, bias=neg_bu[:, 0:1], scale=-1.0).then_inc(g_exp, 1)

            def step(m, j, n):
                if runs(n, 3):
                    wait(act, p_turned, n - 3, 1)
                    wait(act, pv_sum, n - 3)
                    for b in range(2):
                        last = nc.scalar.activation(pT[:, 4 * b:4 * b + 4, :].rearrange("p h q -> p (h q)"),
                                                    ps_pT[:, b, :], ACT.Copy)
                    last.then_inc(pT_ok, 1)
                if j == 0 and older(m, 2):
                    gate_exp(m - 2)
                if ffn_in_window(m):
                    hidden_relu(0, m - 2, 2 * j, bk_f[0])
                if runs(n, 0):
                    wait(act, x_turned, n, 1)
                    wait(act, y_sum, n)
                    nc.scalar.activation(xT_hi[:, :, :], ps_xT, ACT.Copy).then_inc(xT_hi_ok, 1)
                if isinstance(n, int) and n == 0:
                    split_wp()
                for i in parts_in(n):
                    act.wait_ge(ld_we0, 16 if i < PARTS // 2 else 32)
                    nc.scalar.activation(we_hi[0][:, part0(i)], raw_part(i), ACT.Copy).then_inc(we0_hi, 1)
                if ffn_in_window(m):
                    hidden_hi(m - 2, 2 * j, bk_f[0], ha_hi, (m - 2) * KT + 2 * j)
                if runs(n, 0):
                    wait(act, hid_sum, n, 1)
                    wait(act, hid_turned, n)
                    nc.scalar.activation(hid[:, :], ps_h, ACT.Tanh).then_inc(hid_ok, 1)
                if isinstance(n, int) and n == 0:
                    copy_wkv()
                if ffn_in_window(m):
                    hidden_relu(0, m - 2, 2 * j + 1, bank_of(m, 2 * j + 1))
                if runs(n, 4):
                    wait(act, xn2_turned, n - 4, 1)
                    nc.scalar.activation(
                        x2_hi[:, :, bass.ds(ROWS * (n - 4), ROWS)].rearrange("p k (b t) -> p k b t", b=2),
                        ps_x2T.rearrange("p (k b t) -> p k b t", k=KD, b=2)[:, :, :, 0:S], ACT.Copy).then_inc(x2_hi_ok, 1)
                if ffn_in_window(m):
                    hidden_hi(m - 2, 2 * j + 1, bank_of(m, 2 * j + 1), ha_hi, (m - 2) * KT + (2 * j + 1))
                if runs(n, 0):
                    wait(act, hid_turned, n, 1)
                    nc.scalar.activation(xT_hi[:, :, :], ps_hT, ACT.Copy).then_inc(hidT_hi_ok, 1)
                if isinstance(n, int) and n == 0:
                    copy_wkvd()
                if runs(n, 2):
                    wait(act, sc_shifted, n - 2, 1)
                    nc.scalar.activation(probs[:, :, 0:S], probs[:, :, 0:S], ACT.Exp).then_inc(probs_ok, 1)
                if runs(n, 2):
                    wait(act, v_sum, n - 2, 1)
                    wait(act, pv_sum, n - 2)
                    pv = ps_v.rearrange("p (h e d) -> p h e d", h=HEADS // 2, e=2)
                    for clip in range(2):
                        for par in range(2):
                            last = nc.scalar.activation(
                                v_bd[HALF * par:HALF * (par + 1), :, clip, par, :],
                                pv[HALF * clip:HALF * (clip + 1), :, par, :], ACT.Copy)
                    last.then_inc(v_ok, 1)
                if runs(n, 1):
                    wait(act, xn_turned, n - 1, 1)
                    wait(act, q_sum, n - 1)
                    nc.scalar.activation(xnT[:, :, :].rearrange("p k c -> p (k c)"), ps_xnT, ACT.Copy).then_inc(xnT_ok, 1)
                if runs(n, 3):
                    wait(act, o_turned, n - 3, 1)
                    wait(act, at_sum, n - 3)
                    nc.scalar.activation(oT[:, :, :].rearrange("p k c -> p (k c)"), ps_oT, ACT.Copy).then_inc(oT_ok, 1)
                if runs(n, 1):
                    wait(act, lat_sum, n - 1, 1)
                    wait(act, v_sum, n - 1)
                    wait(act, k_sum, n - 1)
                    nc.scalar.activation(latT[:, :], ps_lat, ACT.Copy).then_inc(lat_ok, 1)
                    wait(act, k_sum, n - 1, 1)
                    wait(act, k_exp_ok, n - 1)
                    for odd in range(2):
                        for clip in range(2):
                            last = nc.scalar.activation(
                                k_cp[HALF * clip:HALF * (clip + 1), odd::2, :],
                                ps_k[HALF * odd:HALF * (odd + 1), :, HALF * clip:HALF * clip + S], ACT.Copy)
                    last.then_inc(k_cp_ok, 1)
                    wait(act, q_sum, n - 1, 1)
                    wait(act, sc_sum, n - 1)
                    for odd in range(2):
                        for clip in range(2):
                            last = nc.scalar.activation(
                                q_bd[HALF * clip:HALF * (clip + 1), odd::2, HALF * clip:HALF * (clip + 1)],
                                ps_q[HALF * odd:HALF * (odd + 1), :, HALF * clip:HALF * (clip + 1)], ACT.Copy)
                    last.then_inc(q_ok, 1)

            steps(act, step)
            gate_exp(CHUNKS - 1)
            act.wait_ge(at_sum, TILES)
            act.wait_ge(xn2_turned, TILES)
            act.wait_ge(g_exp, CHUNKS)
            act.wait_ge(w_ok, CHUNKS)

            def split_next(e, c):
                part = bass.ds(PREP * c, PREP)
                act.wait_ge(ld_we, 32 * (e + 1))
                if e:
                    act.wait_ge(f2_sum, KT * CHUNKS * e)
                nc.scalar.activation(we_hi[(e + 1) % 2][:, part], we_raw[:, part], ACT.Copy).then_inc(we_hi_ok, 1)

            def chunk(e, c):
                g = c + CHUNKS * e
                for f in range(KT):
                    bank = bk_f[f % 3]
                    hidden_relu(e, g, f, bank)
                    hidden_hi(g, f, bank, h_hi[:, f % 4, :, :], g * KT + (f - 3) if f >= 4 or e else 0)
                    if e == 0:
                        split_next(0, f)
                    if f == KT - 3 and 0 < e < EXPERTS - 1:
                        split_next(e, c)

            chunks(act, chunk)

        @block.vector
        def _(dve):
            for k in range(KF):
                dve.wait_ge(setup_hi, k + 1)
                nc.vector.tensor_tensor(wdT_lo[:, k, :], psum[:, k, :], wdT_hi[:, k, :].bitcast(F32), ALU.subtract).then_inc(setup_lo, 1)

            def split_wp():
                for k in range(KF // 2):
                    dve.wait_ge(setup_hi, KF + k + 1)
                    nc.vector.tensor_tensor(wpT_lo[:, 2 * k:2 * k + 2, :].rearrange("p a d -> p (a d)"), psum[:, wp_bank[k], :],
                                            wpT_hi[:, 2 * k:2 * k + 2, :].rearrange("p a d -> p (a d)").bitcast(F32), ALU.subtract).then_inc(setup_lo, 1)
                dve.wait_ge(ld_kv, 32)
                nc.vector.tensor_tensor(wkv[:, :, :].rearrange("p a b -> p (a b)"), wk_raw, wv_raw, ALU.add).then_inc(wkv_sum, 1)

            def hidden_lo(g, f, bank, hi, lo):
                dve.wait_ge(h_hi_ok, g * KT + (f + 1))
                nc.vector.tensor_tensor(lo[:, :, 0:S], clips_of(bank), hi[:, :, 0:S].bitcast(F32), ALU.subtract).then_inc(h_lo_ok, 1)

            def weight(e, t):
                return w_gate[:, e, :][:, bass.ds(t, 1)]

            def add_output(e, c, g):
                dve.wait_ge(b2_added, g * TPC + TPC)
                dve.wait_ge(f2_sum, g * KT + KT)
                for j in range(TPC):
                    t = tile_rows(c * TPC + j)
                    nc.vector.scalar_tensor_tensor(out=t, in0=ps_e[:, j, :], scalar=weight(e, c * TPC + j), in1=t,
                                                   op0=ALU.mult, op1=ALU.add).then_inc(y_added, 1)

            def add_bias(e, t, g):
                if not isinstance(g, int) or g > 0:
                    dve.wait_ge(y_added, g * TPC)
                nc.vector.scalar_tensor_tensor(out=tile_rows(t), in0=b2_b[:, e, :], scalar=weight(e, t), in1=tile_rows(t),
                                               op0=ALU.mult, op1=ALU.add).then_inc(b2_added, 1)

            def gate_weights(c):
                dve.wait_ge(g_exp, c + 1)
                nc.vector.tensor_scalar(u_den[:, :], u_exp[:, :], 1.0, None, ALU.add).then_inc(g_step, 1)
                dve.wait_ge(g_step, c * 3 + 2)
                nc.vector.reciprocal(u[:, :], u_den[:, :]).then_inc(g_step, 1)
                dve.wait_ge(g_step, c * 3 + 3)
                for e in range(EXPERTS):
                    last = nc.vector.tensor_scalar(w_step[:, e, :], u[:, :], gate[:, e:e + 1],
                                                   gate[:, EXPERTS + e:EXPERTS + e + 1], ALU.is_gt, ALU.mult)
                last.then_inc(g_step, 1)
                dve.wait_ge(g_step, c * 3 + 4)
                nc.vector.tensor_tensor(w_gate[:, :, bass.ds(c * TPC, TPC)], w_step[:, :, :],
                                        u[:, :].unsqueeze(1).broadcast_to([P, EXPERTS, TPC]), ALU.mult).then_inc(w_ok, 1)

            def step(m, j, n):
                if isinstance(n, int) and n == 1:
                    dve.wait_ge(ld_small, N_SMALL * 16)
                    nc.vector.tensor_scalar(neg_bu[:, :], neg_bu[:, :], -1.0, None, ALU.mult).then_inc(g_step, 1)
                if runs(n, 1):
                    wait(dve, y_rstd_ok, n - 1, 1)
                    if isinstance(n, int) and n == 1:
                        dve.wait_ge(setup_hi, N_SPLIT + 3)
                        dve.wait_ge(setup_pe, N_SPLIT + 2)
                    nc.vector.tensor_scalar(tile_rows(n - 1), ps_y, y_mv[:, 0:1], y_rstd[:, 0:1],
                                            ALU.subtract, ALU.mult).then_inc(y_normed, 1)
                if j == 0 and older(m, 3):
                    add_output(0, m - 3, m - 3)
                if runs(n, 4):
                    wait(dve, h1_ok, n - 4, 1)
                if runs(n, 0):
                    wait(dve, xT_hi_ok, n, 1)
                    nc.vector.tensor_tensor(xT_lo[:, :, :], ps_xT, xT_hi[:, :, :].bitcast(F32), ALU.subtract).then_inc(xT_lo_ok, 1)
                if isinstance(n, int) and n == 0:
                    split_wp()
                if runs(n, 4):
                    nc.vector.bn_stats(h1_stats[:, :], tile_rows(n - 4)).then_inc(h1_st_ok, 1)
                    wait(dve, h1_st_ok, n - 4, 1)
                if ffn_in_window(m):
                    hidden_lo(m - 2, 2 * j, bk_f[0], ha_hi, ha_lo)
                if runs(n, 4):
                    nc.vector.bn_aggr(h1_mv[:, :], h1_stats[:, :]).then_inc(h1_mv_ok, 1)
                if runs(n, 2):
                    wait(dve, sc_sum, n - 2, 1)
                    nc.vector.tensor_scalar(ps_sc, ps_sc, -CLAMP * SCALE_INV, CLAMP * SCALE_INV,
                                            ALU.max, ALU.min).then_inc(sc_clipped, 1)
                if runs(n, 4):
                    wait(dve, h1_rstd_ok, n - 4, 1)
                    wait(dve, xn2_turned, n - 4)
                    nc.vector.tensor_scalar(xn2[:, :], tile_rows(n - 4), h1_mv[:, 0:1], h1_rstd[:, 0:1],
                                            ALU.subtract, ALU.mult).then_inc(xn2_ok, 1)
                if runs(n, 1):
                    wait(dve, h0_ok, n - 1, 1)
                if runs(n, 2):
                    wait(dve, sc_clipped, n - 2, 1)
                    nc.vector.tensor_tensor(ps_sc_h, ps_sc_h,
                                            decay[:, :].unsqueeze(1).unsqueeze(1).broadcast_to([P, 2, 2 * HPQ, S]),
                                            ALU.mult).then_inc(sc_decayed, 1)
                if runs(n, 1):
                    nc.vector.bn_stats(h0_stats[:, :], tile_rows(n - 1)).then_inc(h0_st_ok, 1)
                    wait(dve, h0_st_ok, n - 1, 1)
                if runs(n, 2):
                    wait(dve, sc_decayed, n - 2, 1)
                    nc.vector.tensor_reduce(row_max[:, :].rearrange("p (b h) -> p b h", b=2), ps_sc_h, AX.X, ALU.max).then_inc(max_ok, 1)
                if runs(n, 1):
                    nc.vector.bn_aggr(h0_mv[:, :], h0_stats[:, :]).then_inc(h0_mv_ok, 1)
                if runs(n, 2):
                    wait(dve, max_ok, n - 2, 1)
                    wait(dve, p_turned, n - 2)
                    nc.vector.tensor_tensor(
                        probs[:, :, 0:S].rearrange("p (b h) k -> p b h k", b=2), ps_sc_h,
                        row_max[:, :].rearrange("p (b h) -> p b h", b=2).unsqueeze(3).broadcast_to([P, 2, 2 * HPQ, S]),
                        ALU.subtract).then_inc(sc_shifted, 1)
                if ffn_in_window(m):
                    hidden_lo(m - 2, 2 * j + 1, bank_of(m, 2 * j + 1), ha_hi, ha_lo)
                if runs(n, 4):
                    wait(dve, x2_hi_ok, n - 4, 1)
                    cols = bass.ds(ROWS * (n - 4), ROWS)
                    nc.vector.tensor_tensor(
                        x2_lo[:, :, cols].rearrange("p k (b t) -> p k b t", b=2),
                        ps_x2T.rearrange("p (k b t) -> p k b t", k=KD, b=2)[:, :, :, 0:S],
                        x2_hi[:, :, cols].rearrange("p k (b t) -> p k b t", b=2).bitcast(F32),
                        ALU.subtract).then_inc(x2_lo_ok, 1)
                if runs(n, 3):
                    wait(dve, pv_sum, n - 3, 1)
                    wait(dve, inv_ok, n - 3, 1)
                    wait(dve, o_turned, n - 3)
                    for clip in range(2):
                        rows = slice(HALF * clip, HALF * (clip + 1))
                        last = nc.vector.tensor_tensor(
                            o_sb[rows, :, :].rearrange("p (h e) d -> p h e d", e=2), ps_pv[rows, :, clip, :, :],
                            row_inv[rows, :].rearrange("p (h e) -> p h e", e=2).unsqueeze(3).broadcast_to([HALF, HEADS // 2, 2, DH]),
                            ALU.mult)
                    last.then_inc(o_ok, 1)
                if runs(n, 1):
                    wait(dve, h0_rstd_ok, n - 1, 1)
                    wait(dve, xn_turned, n - 1)
                    nc.vector.tensor_scalar(xn[:, :], tile_rows(n - 1), h0_mv[:, 0:1], h0_rstd[:, 0:1],
                                            ALU.subtract, ALU.mult).then_inc(xn_ok, 1)
                if runs(n, 0):
                    wait(dve, hidT_hi_ok, n, 1)
                    nc.vector.tensor_tensor(xT_lo[:, :, :], ps_hT, xT_hi[:, :, :].bitcast(F32), ALU.subtract).then_inc(hidT_lo_ok, 1)
                if runs(n, 4):
                    wait(dve, xn2_ok, n - 4, 1)
                    if j == 0 and older(m, 2):
                        dve.wait_ge(g_exp, m - 1)
                    nc.vector.tensor_tensor_reduce(logit_terms[:, :], xn2[:, :], wu_b[:, :], 1.0, 0.0, ALU.mult, ALU.add,
                                                   logit[:, j:j + 1]).then_inc(logit_ok, 1)
                if j == 0 and older(m, 2):
                    gate_weights(m - 2)
                if ffn_in_window(m):
                    if j == 0:
                        dve.wait_ge(w_ok, m - 1)
                    add_bias(0, (m - 2) * TPC + j, m - 2)
                if runs(n, 2):
                    wait(dve, probs_ok, n - 2, 1)
                    nc.vector.tensor_reduce(row_sum[:, :], probs[:, :, 0:S], AX.X, ALU.add).then_inc(sum_ok, 1)
                if runs(n, 0):
                    wait(dve, y_sum, n, 1)
                    nc.vector.bn_stats(y_stats[:, :], ps_y).then_inc(y_st_ok, 1)
                    wait(dve, y_st_ok, n, 1)
                if runs(n, 2):
                    wait(dve, sum_ok, n - 2, 1)
                    nc.vector.reciprocal(row_inv[:, :], row_sum[:, :]).then_inc(inv_ok, 1)
                if runs(n, 0):
                    nc.vector.bn_aggr(y_mv[:, :], y_stats[:, :]).then_inc(y_mv_ok, 1)
                if runs(n, 3):
                    wait(dve, at_sum, n - 3, 1)
                    nc.vector.tensor_tensor(tile_rows(n - 3), ps_at, tile_rows(n - 3), ALU.add).then_inc(h1_ok, 1)

            steps(dve, step)
            gate_weights(CHUNKS - 1)
            dve.wait_ge(at_sum, TILES)
            dve.wait_ge(xn2_turned, TILES)

            def chunk(e, c):
                g = c + CHUNKS * e
                if e and isinstance(c, int):
                    add_output(e - 1, CHUNKS - 1, g - 1)
                else:
                    add_output(e, c - 1, g - 1)
                for f in range(KT):
                    hidden_lo(g, f, bk_f[f % 3], h_hi[:, f % 4, :, :], h_lo[:, f % 4, :, :])
                    if f >= TPC:
                        add_bias(e, c * TPC + (f - TPC), g)

            chunks(dve, chunk)
            add_output(EXPERTS - 1, CHUNKS - 1, CHUNKS * EXPERTS - 1)

        @block.tensor
        def _(pe):
            pe.wait_ge(ld_ident, 16)
            pe.wait_ge(ld_wd, 32)
            for k in range(KF):
                for g in range(KF):
                    last = nc.tensor.transpose(psum[:, k, g * P:(g + 1) * P], wd_raw[:, g, k * P:(k + 1) * P], ident[:, :])
                last.then_inc(setup_pe, 1)
            def turn_wp():
                pe.wait_ge(ld_wp, 16)
                for k2 in range(KF // 2):
                    for i in range(2):
                        for d in range(KD):
                            k = 2 * k2 + i
                            last = nc.tensor.transpose(psum[:, wp_bank[k2], (KD * i + d) * P:(KD * i + d + 1) * P],
                                                       wp_raw[:, d, k * P:(k + 1) * P], ident[:, :])
                    last.then_inc(setup_pe, 1)

            def turn_wkv():
                pe.wait_ge(setup_lo, N_SPLIT)
                pe.wait_ge(wkv_sum, 1)
                pe.wait_ge(ld_b1, 16)
                for j in range(KD):
                    for i in range(KD):
                        nc.tensor.transpose(psum[:, 6, (KD * j + i) * P:(KD * j + i + 1) * P], wkv[:, i, j * P:(j + 1) * P], ident[:, :])
                nb = EXPERTS * KT
                nc.tensor.transpose(psum[:, 7, 0:nb], b1_raw[0:nb, :], ident[0:nb, 0:nb]).then_inc(setup_pe, 1)

            def project_wkv():
                pe.wait_ge(setup_hi, N_SPLIT + 2)
                pe.wait_ge(ld_down, 16)
                for i in range(KD):
                    for j in range(KD):
                        last = nc.tensor.matmul(psum[:, 7, 128 + i * LAT:128 + (i + 1) * LAT], wkvT[:, j, i * P:(i + 1) * P],
                                                wdown[:, j, :], start=(j == 0), stop=(j == KD - 1))
                last.then_inc(setup_pe, 1)

            def split_product(dst, lhs_hi, lhs_lo, rhs_hi, rhs_lo, first, last):
                nc.tensor.matmul(dst, lhs_hi, rhs_hi, start=first, stop=False)
                nc.tensor.matmul(dst, lhs_hi, rhs_lo, start=False, stop=False)
                return nc.tensor.matmul(dst, lhs_lo, rhs_hi, start=False, stop=last)

            def first_layer(e, g, c, f, bank, free):
                if not isinstance(free, int) or free > 0:
                    pe.wait_ge(h_lo_ok, free)
                w_hi = we_hi[e % 2][:, 0:WCOLS].rearrange("p (k f) -> p k f", k=KD)
                w_lo = we_lo[e % 2][:, 0:WCOLS].rearrange("p (k f) -> p k f", k=KD)
                cols, feats = bass.ds(c * CW, CW), slice(f * P, (f + 1) * P)
                for k in range(KD):
                    last = split_product(psum[:, bank, 0:CW], w_hi[:, k, feats], w_lo[:, k, feats],
                                         x2_hi[:, k, cols], x2_lo[:, k, cols], k == 0, k == KD - 1)
                last.then_inc(f1_sum, 1)

            def rows_of(h, j):
                return h[:, 2 * j:2 * j + 2, :].rearrange("p b t -> p (b t)")

            def second_layer(e, g, f, hi, lo):
                pe.wait_ge(h_lo_ok, g * KT + (f + 1))
                if f == 0 and (not isinstance(g, int) or g > 0):
                    pe.wait_ge(y_added, g * TPC)
                w_hi = we_hi[e % 2][:, WCOLS:].rearrange("p (k d) -> p k d", k=KT)
                w_lo = we_lo[e % 2][:, WCOLS:].rearrange("p (k d) -> p k d", k=KT)
                for j in range(TPC):
                    last = split_product(ps_e[:, j, :], rows_of(hi, j), rows_of(lo, j), w_hi[:, f, :], w_lo[:, f, :],
                                         f == 0 and j % 2 == 0, f == KT - 1 and j % 2 == 1)
                last.then_inc(f2_sum, 1)

            def step(m, j, n):
                ffn, g = ffn_in_window(m), m - 2
                if isinstance(n, int) and n == 1:
                    pe.wait_ge(setup_hi, N_SPLIT + 3)
                    pe.wait_ge(ld_att, 32)
                    pe.wait_ge(ld_up, 32)
                if runs(n, 3):
                    wait(pe, probs_ok, n - 3, 1)
                    wait(pe, lat_ok, n - 2, 1)
                    wait(pe, v_ok, n - 3, 1)
                    for h in range(HEADS // 2):
                        if h == HPQ:
                            wait(pe, k_cp_ok, n - 2, 1)
                        last = nc.tensor.transpose(ps_pT[:, h // 4, (h % 4) * P:(h % 4 + 1) * P],
                                                   probs[:, 2 * h:2 * h + 2, :].rearrange("p e k -> p (e k)"), ident[:, :])
                    last.then_inc(p_turned, 1)
                if ffn:
                    if isinstance(m, int) and m == 2 and j == 0:
                        pe.wait_ge(we0_lo, PARTS)
                        pe.wait_ge(h_pad, 2)
                    first_layer(0, g, g, 2 * j, bk_f[0], g * KT + 2 * j)
                if runs(n, 0):
                    wait(pe, x_loaded, n, 1, 64)
                    wait(pe, q_ok, n - 1)
                    for k in range(KF):
                        last = nc.tensor.transpose(ps_xT[:, k, :], x_sb[:, k * P:(k + 1) * P], ident[:, :])
                    last.then_inc(x_turned, 1)
                if isinstance(n, int) and n == 0:
                    turn_wp()
                    pe.wait_ge(setup_lo, KF)
                    pe.wait_ge(bias_h, 1)
                    pe.wait_ge(bias_done, 2)
                if runs(n, 2):
                    wait(pe, q_ok, n - 2, 1)
                    wait(pe, k_exp_ok, n - 2, 1)
                    if runs(n, 3):
                        wait(pe, pT_ok, n - 3, 1)
                    for c in range(QUADS):
                        last = nc.tensor.matmul(ps_sc[:, c // 2, (c % 2) * HPQ * S:(c % 2 + 1) * HPQ * S], q_bd[:, c, :],
                                                k_exp[:, c, :, :].rearrange("p h k -> p (h k)"), start=True, stop=True)
                    last.then_inc(sc_sum, 1)
                if runs(n, 0):
                    wait(pe, xT_lo_ok, n, 1)
                    wait(pe, y_normed, n)
                    nc.tensor.matmul(ps_h, ones[:, :], bias2[:, 0:F2D], start=True, stop=False)
                    for k in range(KF):
                        last = split_product(ps_h, xT_hi[:, k, :], xT_lo[:, k, :], wdT_hi[:, k, :], wdT_lo[:, k, :],
                                             False, k == KF - 1)
                    last.then_inc(hid_sum, 1)
                if isinstance(n, int) and n == 0:
                    turn_wkv()
                if ffn:
                    if drains(m) and j == 0:
                        pe.wait_ge(y_normed, TILES)
                    first_layer(0, g, g, 2 * j + 1, bank_of(m, 2 * j + 1), g * KT + (2 * j + (0 if drains(m) else 1)))
                    if drains(m):
                        second_layer(0, g, 2 * j, ha_hi, ha_lo)
                if runs(n, 4):
                    wait(pe, xn2_ok, n - 4, 1)
                    if runs(n, 0):
                        wait(pe, xT_lo_ok, n, 1)
                    for k in range(KD):
                        last = nc.tensor.transpose(ps_x2T[:, k * P:(k + 1) * P], xn2[:, k * P:(k + 1) * P], ident[:, :])
                    last.then_inc(xn2_turned, 1)
                if ffn and not drains(m):
                    second_layer(0, g, 2 * j, ha_hi, ha_lo)
                if runs(n, 3):
                    wait(pe, pT_ok, n - 3, 1)
                    wait(pe, v_ok, n - 3, 1)
                    wait(pe, h1_ok, n - 4, 1)
                    for h in range(HEADS // 2):
                        last = nc.tensor.matmul(ps_pv[:, h, :, :, :].rearrange("p b e d -> p (b e d)"), pT[:, h, :],
                                                v_bd[:, h, :, :, :].rearrange("p b e d -> p (b e d)"), start=True, stop=True)
                    last.then_inc(pv_sum, 1)
                if runs(n, 0):
                    wait(pe, hid_ok, n, 1)
                    for k in range(KF):
                        last = nc.tensor.transpose(ps_hT[:, k, :], hid[:, k * P:(k + 1) * P], ident[:, :])
                    last.then_inc(hid_turned, 1)
                if isinstance(n, int) and n == 0:
                    project_wkv()
                if ffn:
                    second_layer(0, g, 2 * j + 1, ha_hi, ha_lo)
                if runs(n, 2):
                    wait(pe, lat_ok, n - 2, 1)
                    wait(pe, sc_shifted, n - 2, 1)
                    nc.tensor.matmul(ps_v, latT[:, :], wup[:, D:], start=True, stop=True).then_inc(v_sum, 1)
                if runs(n, 1):
                    wait(pe, xn_ok, n - 1, 1)
                    if runs(n, 4):
                        wait(pe, x2_lo_ok, n - 4, 1)
                    elif runs(n, 0):
                        wait(pe, xT_lo_ok, n, 1)
                    for k in range(KD):
                        last = nc.tensor.transpose(ps_xnT[:, k * P:(k + 1) * P], xn[:, k * P:(k + 1) * P], ident[:, :])
                    last.then_inc(xn_turned, 1)
                if runs(n, 3):
                    wait(pe, o_ok, n - 3, 1)
                    for k in range(KD):
                        last = nc.tensor.transpose(ps_oT[:, k * P:(k + 1) * P],
                                                   o_sb[:, k * P // DH:(k + 1) * P // DH, :].rearrange("p h d -> p (h d)"), ident[:, :])
                    last.then_inc(o_turned, 1)
                if runs(n, 0):
                    wait(pe, hidT_lo_ok, n, 1)
                    nc.tensor.matmul(ps_y, ones[:, :], bias2[:, F2D:], start=True, stop=False)
                    for k in range(KF):
                        last = split_product(ps_y, xT_hi[:, k, :], xT_lo[:, k, :], wpT_hi[:, k, :], wpT_lo[:, k, :],
                                             False, k == KF - 1)
                    last.then_inc(y_sum, 1)
                if runs(n, 1):
                    wait(pe, xnT_ok, n - 1, 1)
                    for k in range(KD):
                        last = nc.tensor.matmul(ps_lat, wkvd[:, k, :], xnT[:, k, :], start=(k == 0), stop=(k == KD - 1))
                    last.then_inc(lat_sum, 1)
                if runs(n, 3):
                    wait(pe, oT_ok, n - 3, 1)
                    for k in range(KD):
                        last = nc.tensor.matmul(ps_at, oT[:, k, :], wo[:, k, :], start=(k == 0), stop=(k == KD - 1))
                    last.then_inc(at_sum, 1)
                if runs(n, 1):
                    wait(pe, lat_ok, n - 1, 1)
                    wait(pe, v_ok, n - 2, 1)
                    for q in range(KD):
                        last = nc.tensor.matmul(ps_k[:, q, :], wup[:, q * P:(q + 1) * P], latT[:, :], start=True, stop=True)
                    last.then_inc(k_sum, 1)
                    for q in range(KD):
                        for k in range(KD):
                            last = nc.tensor.matmul(ps_q[:, q, :], wq[:, k, q * P:(q + 1) * P], xnT[:, k, :],
                                                    start=(k == 0), stop=(k == KD - 1))
                    last.then_inc(q_sum, 1)

            steps(pe, step)
            pe.wait_ge(h1_ok, TILES)
            pe.wait_ge(x2_lo_ok, TILES)
            pe.wait_ge(y_normed, TILES)
            pe.wait_ge(h_pad, 4)

            def chunk(e, c):
                g = c + CHUNKS * e
                if e:
                    pe.wait_ge(we_lo_ok, CHUNKS * e)
                for f in range(3):
                    first_layer(e, g, c, f, bk_f[f], g * KT)
                for f in range(KT):
                    second_layer(e, g, f, h_hi[:, f % 4, :, :], h_lo[:, f % 4, :, :])
                    if f + 3 < KT:
                        first_layer(e, g, c, f + 3, bk_f[f % 3], g * KT + (f + 1))

            chunks(pe, chunk)


_INS = ['x', 'L0_tok_Wd', 'L0_tok_bd', 'L0_tok_Wp', 'L0_tok_bp', 'L0_tok_gamma', 'L0_tok_beta', 'L0_attn_Wq',
        'L0_attn_Wk', 'L0_attn_Wv', 'L0_attn_Wo', 'L0_attn_W_down_kv', 'L0_attn_W_up_k', 'L0_attn_W_up_v',
        'L0_ffn_W1', 'L0_ffn_b1', 'L0_ffn_W2', 'L0_ffn_b2', 'L0_ffn_Wu', 'L0_ffn_bu']
_OUT = (CLIPS, S, D)


def constants():
    import numpy as np
    row = np.arange(P) % HALF
    decay = np.exp(np.float32(-0.01 * 0.01) * np.abs(row[:, None] - np.arange(S)[None, :]).astype(np.float32))
    headmask = (row[:, None] // DH == np.arange(HPQ)[None, :]).astype(np.float32)
    step = (np.arange(EXPERTS)[None, :] - row[:, None]) % EXPERTS + 1
    gate = np.concatenate([np.where(step == 1, -1.0, (step - 1) / EXPERTS), 1.0 / step], axis=1)
    return {"c_ident": np.eye(P, dtype=np.float32), "c_decay": (decay / np.float32(SCALE_INV)).astype(np.float32),
            "c_headmask": headmask, "c_gate": gate.astype(np.float32)}


def kernel(**inputs):
    import numpy as _np
    import concourse.bacc as _bacc
    from concourse import mybir as _mybir
    from concourse.bass_utils import run_bass_kernel_spmd as _run

    nc = _bacc.Bacc("TRN2", target_bir_lowering=False, num_devices=1)
    arrays, args = {}, []
    tables = constants()
    for name in _INS + list(tables):
        a = _np.ascontiguousarray(tables[name] if name in tables else inputs[name])
        arrays[f"in_{name}_dram"] = a
        args.append(nc.dram_tensor(f"in_{name}_dram", a.shape, _mybir.dt.from_np(a.dtype), kind="ExternalInput").ap())
    args.append(nc.dram_tensor("out_0_dram", _OUT, F32, kind="ExternalOutput").ap())
    build(nc, *args)
    r = _run(nc, [arrays], core_ids=[0])
    return r.results[0]["out_0_dram"]
```

```python
from contextlib import ExitStack

import concourse.bass as bass
from concourse import mybir

F32 = mybir.dt.float32
F32R = mybir.dt.float32r
ALU = mybir.AluOpType
ACT = mybir.ActivationFunctionType
AX = mybir.AxisListType

P = 128
CLIPS, FRAMES, D = 64, 125, 256
S = FRAMES // 2
HALF = 64
TILES = CLIPS // 2
ROWS = 2 * S
F2D = 2 * D
HEADS, DH, LAT = 16, 16, 64
QUADS, HPQ = 4, 4
FF, EXPERTS = 1024, 4
KD, KF, KT = D // P, F2D // P, FF // P
CHUNKS, TPC = 8, TILES // 8
CW = TPC * ROWS
LN_EPS = 1e-5
CLAMP = 10000.0
SCALE_INV = 16.0
LAST_LAG = 4
PEELED = 3
WCOLS = KD * FF
PREP = 2 * WCOLS // CHUNKS


def build(nc, x, Wd, bd, Wp, bp, gamma, beta, Wq, Wk, Wv, Wo, Wdown, Wupk, Wupv,
          W1, b1, W2, b2, Wu, bu, c_ident, c_decay, c_headmask, c_gate, out):
    ctx = ExitStack()
    with ctx:
        def sem(name):
            return ctx.enter_context(nc.semaphore(name))

        def sb(name, shape, dt=F32, stack=None):
            return (stack or ctx).enter_context(nc.sbuf_tensor(name, shape, dt))

        x2_hi = sb("x2_hi", [P, KD, TILES * ROWS], F32R)
        x2_lo = sb("x2_lo", [P, KD, TILES * ROWS], F32R)
        resid = sb("resid", [P, TILES, D])
        we_hi = [sb("we_hi0", [P, 2 * WCOLS], F32R)]
        we_lo = [sb("we_lo0", [P, 2 * WCOLS], F32R)]
        ident = sb("ident_sb", [P, P])
        b1T = sb("b1T", [P, EXPERTS * KT])
        b2_b = sb("b2_b", [P, EXPERTS, D])
        gate = sb("gate", [P, 2 * EXPERTS])
        logit = sb("logit", [P, TPC])
        u_exp = sb("u_exp", [P, TPC])
        u_den = sb("u_den", [P, TPC])
        u = sb("u", [P, TPC])
        w_step = sb("w_step", [P, EXPERTS, TPC])
        neg_bu = sb("neg_bu", [P, 1])
        eps = sb("eps", [P, 1])
        tick = sb("tick", [P, 1])
        w_gate = sb("w_gate", [P, EXPERTS, TILES])
        psum = ctx.enter_context(nc.psum_tensor("psum", [P, 8, 512], F32))

        scratch = resid[:, :, :].rearrange("p t d -> p (t d)")
        used = [0]

        def stage(cols):
            used[0] += cols
            return scratch[:, used[0] - cols:used[0]]

        wd_raw = stage(KF * F2D).rearrange("p (a b) -> p a b", a=KF)
        wp_raw = stage(KD * F2D).rearrange("p (a b) -> p a b", a=KD)
        wk_raw = stage(KD * D)
        wv_raw = stage(KD * D)
        wkv = stage(KD * D).rearrange("p (a b) -> p a b", a=KD)
        wkvT = stage(KD * D).rearrange("p (a b) -> p a b", a=KD)
        wdown = stage(KD * LAT).rearrange("p (a b) -> p a b", a=KD)
        b1_raw = stage(P)
        we_raw0 = stage(WCOLS)
        bias_raw = stage(F2D + D)
        assert used[0] <= TILES * D

        pa = ExitStack()
        wdT_hi = sb("wdT_hi", [P, KF, F2D], F32R, pa)
        wdT_lo = sb("wdT_lo", [P, KF, F2D], F32R, pa)
        wpT_hi = sb("wpT_hi", [P, KF, D], F32R, pa)
        wpT_lo = sb("wpT_lo", [P, KF, D], F32R, pa)
        ha_hi = sb("ha_hi", [P, 2 * TPC, HALF], F32R, pa)
        ha_lo = sb("ha_lo", [P, 2 * TPC, HALF], F32R, pa)
        wq = sb("wq", [P, KD, D], stack=pa)
        wo_hi = sb("wo_hi", [P, KD, D], F32R, pa)
        wo_lo = sb("wo_lo", [P, KD, D], F32R, pa)
        wkvd = sb("wkvd", [P, KD, LAT], stack=pa)
        wupk = sb("wupk", [LAT, D], stack=pa)
        halves = sb("halves", [P, F2D + D], F32R, pa)
        bias2 = halves[HALF:P, :]
        wupv_hi, wupv_lo = halves[0:LAT, 0:D], halves[0:LAT, D:2 * D]
        ones = sb("ones", [P, P], F32R, pa)
        gamma_b = sb("gamma_b", [P, D], stack=pa)
        beta_b = sb("beta_b", [P, D], stack=pa)
        wu_b = sb("wu_b", [P, D], stack=pa)
        decay = sb("decay", [P, S], stack=pa)
        headmask = sb("headmask", [P, HPQ], stack=pa)
        neg_half = sb("neg_half", [P, 1], stack=pa)
        x_sb = sb("x_sb", [P, F2D], stack=pa)
        xT_hi = sb("xT_hi", [P, KF, P], F32R, pa)
        xT_lo = sb("xT_lo", [P, KF, P], F32R, pa)
        hid = sb("hid", [P, F2D], stack=pa)
        y_stats = sb("y_stats", [P, 6], stack=pa)
        y_mv = sb("y_mv", [P, 2], stack=pa)
        y_ve = sb("y_ve", [P, 1], stack=pa)
        y_rstd = sb("y_rstd", [P, 1], stack=pa)
        h0_stats = sb("h0_stats", [P, 6], stack=pa)
        h0_mv = sb("h0_mv", [P, 2], stack=pa)
        h0_ve = sb("h0_ve", [P, 1], stack=pa)
        h0_rstd = sb("h0_rstd", [P, 1], stack=pa)
        h1_stats = sb("h1_stats", [P, 6], stack=pa)
        h1_mv = sb("h1_mv", [P, 2], stack=pa)
        h1_ve = sb("h1_ve", [P, 1], stack=pa)
        h1_rstd = sb("h1_rstd", [P, 1], stack=pa)
        xn = sb("xn", [P, D], stack=pa)
        xnT = sb("xnT", [P, KD, P], stack=pa)
        latT = sb("latT", [LAT, P], stack=pa)
        latT_hi = sb("latT_hi", [LAT, P], F32R, pa)
        latT_lo = sb("latT_lo", [LAT, P], F32R, pa)
        q_bd = sb("q_bd", [P, QUADS, P], stack=pa)
        k_cp = sb("k_cp", [P, QUADS, S], stack=pa)
        k_exp = sb("k_exp", [P, QUADS, HPQ, S], stack=pa)
        v_bd = sb("v_bd", [P, HEADS // 2, 2, 2, DH], stack=pa)
        row_max = sb("row_max", [P, HEADS], stack=pa)
        row_sum = sb("row_sum", [P, HEADS], stack=pa)
        row_inv = sb("row_inv", [P, HEADS], stack=pa)
        probs = sb("probs", [P, HEADS, HALF], stack=pa)
        pT = sb("pT", [P, HEADS // 2, P], stack=pa)
        o_sb = sb("o_sb", [P, HEADS, DH], stack=pa)
        oT_hi = sb("oT_hi", [P, KD, P], F32R, pa)
        oT_lo = sb("oT_lo", [P, KD, P], F32R, pa)
        xn2 = sb("xn2", [P, D], stack=pa)
        pa.close()
        pT_flat = pT[:, :, :].rearrange("p h q -> p (h q)")
        wo_raw, wupv_raw = pT_flat[:, 0:KD * D], pT_flat[0:LAT, KD * D:KD * D + D]

        pb = ExitStack()
        we_raw = sb("we_raw", [P, 2 * WCOLS], stack=pb)
        we_hi.append(sb("we_hi1", [P, 2 * WCOLS], F32R, pb))
        we_lo.append(sb("we_lo1", [P, 2 * WCOLS], F32R, pb))
        h_hi = sb("h_hi", [P, 4, 2 * TPC, HALF], F32R, pb)
        h_lo = sb("h_lo", [P, 4, 2 * TPC, HALF], F32R, pb)
        pb.close()

        bk_f, bk_y, bk_s, bk_h, bk_x, bk_o = (0, 5, 6), 1, 3, 5, 6, 7
        ps_xT = psum[:, bk_x, :].rearrange("p (k c) -> p k c", k=KF)
        ps_x2T = psum[:, bk_x, 0:KD * P]
        ps_xnT = psum[:, bk_x, 0:KD * P]
        ps_q = psum[:, bk_x, 0:KD * P].rearrange("p (m c) -> p m c", m=KD)
        ps_lat = psum[0:LAT, bk_s, 0:P]
        ps_sc = psum[:, bk_s:bk_s + 2, 0:2 * HPQ * S]
        ps_sc_h = ps_sc.rearrange("p b (h k) -> p b h k", k=S)
        ps_pT = psum[:, bk_s:bk_s + 2, :]
        ps_h = psum[:, bk_h, :]
        ps_hT = psum[:, bk_h, :].rearrange("p (k c) -> p k c", k=KF)
        ps_y = psum[:, bk_h, 0:D]
        ps_v = psum[:, bk_s + 1, 0:D]
        ps_at = psum[:, bk_o, 0:D]
        ps_oT = psum[:, bk_o, 0:KD * P]
        ps_k = psum[:, bk_s + 1, 0:KD * P].rearrange("p (m c) -> p m c", m=KD)
        ps_pv = psum[:, bk_o, :].rearrange("p (h b e d) -> p h b e d", h=HEADS // 2, b=2, e=2)
        ps_e = psum[:, bk_y:bk_y + 2, :].rearrange("p b (j d) -> p (b j) d", j=2)

        ld_wd = [sem(f"ld_wd{k}") for k in range(KF)]
        ld_ident, ld_wp, ld_kv, ld_down = (sem(s) for s in ("ld_ident", "ld_wp", "ld_kv", "ld_down"))
        ld_att, ld_small, ld_b1, ld_up = (sem(s) for s in ("ld_att", "ld_small", "ld_b1", "ld_up"))
        ld_bias, ld_we0, ld_we = sem("ld_bias"), sem("ld_we0"), sem("ld_we")
        zeroed, wkv_sum, setup_pe, setup_hi, setup_lo = (sem(s) for s in ("zeroed", "wkv_sum", "setup_pe", "setup_hi", "setup_lo"))
        wov_hi, wov_lo, latT_hi_ok, latT_lo_ok, oT_lo_ok = (sem(s) for s in ("wov_hi", "wov_lo", "latT_hi_ok", "latT_lo_ok", "oT_lo_ok"))
        bias_h, bias_done, we0_hi, we0_lo = sem("bias_h"), sem("bias_done"), sem("we0_hi"), sem("we0_lo")
        x_loaded = sem("x_loaded")
        x_turned, xT_hi_ok, xT_lo_ok, hid_sum = sem("x_turned"), sem("xT_hi_ok"), sem("xT_lo_ok"), sem("hid_sum")
        hid_ok, hid_turned, hidT_hi_ok, hidT_lo_ok = sem("hid_ok"), sem("hid_turned"), sem("hidT_hi_ok"), sem("hidT_lo_ok")
        y_sum, y_st_ok, y_mv_ok, y_ve_ok, y_rstd_ok = (sem(s) for s in ("y_sum", "y_st_ok", "y_mv_ok", "y_ve_ok", "y_rstd_ok"))
        y_normed, y_scaled, h0_ok = sem("y_normed"), sem("y_scaled"), sem("h0_ok")
        h0_st_ok, h0_mv_ok, h0_ve_ok, h0_rstd_ok = sem("h0_st_ok"), sem("h0_mv_ok"), sem("h0_ve_ok"), sem("h0_rstd_ok")
        xn_ok, xn_turned, xnT_ok, q_sum = sem("xn_ok"), sem("xn_turned"), sem("xnT_ok"), sem("q_sum")
        lat_ok, q_ok, k_sum, k_cp_ok, k_exp_ok = (sem(s) for s in ("lat_ok", "q_ok", "k_sum", "k_cp_ok", "k_exp_ok"))
        v_sum, v_ok, lat_sum = sem("v_sum"), sem("v_ok"), sem("lat_sum")
        sc_sum, sc_clipped, sc_decayed, max_ok, sc_shifted = (sem(s) for s in ("sc_sum", "sc_clipped", "sc_decayed", "max_ok", "sc_shifted"))
        probs_ok, sum_ok, inv_ok, p_turned, pT_ok = (sem(s) for s in ("probs_ok", "sum_ok", "inv_ok", "p_turned", "pT_ok"))
        pv_sum, o_ok, o_turned, oT_ok, at_sum = (sem(s) for s in ("pv_sum", "o_ok", "o_turned", "oT_ok", "at_sum"))
        h1_ok, h1_st_ok, h1_mv_ok, h1_ve_ok, h1_rstd_ok = (sem(s) for s in ("h1_ok", "h1_st_ok", "h1_mv_ok", "h1_ve_ok", "h1_rstd_ok"))
        xn2_ok, xn2_turned, x2_hi_ok, x2_lo_ok, logit_ok = (sem(s) for s in ("xn2_ok", "xn2_turned", "x2_hi_ok", "x2_lo_ok", "logit_ok"))

        g_exp, g_step, w_ok = sem("g_exp"), sem("g_step"), sem("w_ok")
        f1_sum, h_ok, h_hi_ok, h_lo_ok, f2_sum = (sem(s) for s in ("f1_sum", "h_ok", "h_hi_ok", "h_lo_ok", "f2_sum"))
        h_pad, y_added, b2_added = sem("h_pad"), sem("y_added"), sem("b2_added")
        we_hi_ok, we_lo_ok, stored = sem("we_hi_ok"), sem("we_lo_ok"), sem("stored")

        N_SPLIT = KF + KF // 2
        wp_bank = (4, 7)
        N_SMALL = 8

        def runs(n, lag):
            return not isinstance(n, int) or 0 <= n - lag < TILES

        def wait(eng, s, n, more=0, each=1):
            if isinstance(n, int):
                count = min(n + more, TILES) * each
                if count > 0:
                    eng.wait_ge(s, count)
            else:
                eng.wait_ge(s, (n + more) * each)

        def tile_rows(t):
            return resid[:, bass.ds(t, 1), :].rearrange("p t d -> p (t d)")

        def clips_of(bank):
            return psum[:, bank, 0:CW].rearrange("p (b t) -> p b t", t=S)

        def steps(eng, step):
            for m in range(PEELED):
                for j in range(TPC):
                    step(m, j, TPC * m + j)
            with eng.Fori(PEELED, CHUNKS) as m:
                for j in range(TPC):
                    step(m, j, m * TPC + j)
            for j in range(LAST_LAG):
                step(CHUNKS, j, TILES + j)

        def ffn_in_window(m):
            return not isinstance(m, int) or m >= 2

        PARTS = 2 * TPC

        def parts_in(n):
            return {1: (0, 1), 2: (2, 3), 4: (4,), 5: (5,), 6: (6,), 7: (7,)}.get(n, ()) if isinstance(n, int) else ()

        def part0(n):
            return slice(n * 2 * WCOLS // PARTS, (n + 1) * 2 * WCOLS // PARTS)

        def raw_part(n):
            a = n % (PARTS // 2) * 2 * WCOLS // PARTS
            return we_raw0[:, a:a + 2 * WCOLS // PARTS]

        def drains(m):
            return isinstance(m, int) and m == CHUNKS

        def bank_of(m, f):
            return bk_h if drains(m) and f % 2 else bk_f[0]

        def hidden_of(m, f):
            if drains(m) and f % 2:
                return [t[:, :, :].rearrange("p a b -> p (a b)")[:, 0:TPC * P].rearrange("p (b t) -> p b t", t=HALF)
                        for t in (wpT_hi, wpT_lo)]
            return ha_hi, ha_lo

        def older(m, age):
            return not isinstance(m, int) or m >= age

        def chunks(eng, chunk):
            chunk(0, CHUNKS - 1)
            for e in range(1, EXPERTS):
                chunk(e, 0)
                with eng.Fori(1, CHUNKS) as c:
                    chunk(e, c)

        block = ctx.enter_context(nc.Block())

        @block.sync
        def _(sp):
            sp.dma_start(ident[:, :], c_ident).then_inc(ld_ident, 16)
            for k in range(KF):
                sp.dma_start(wd_raw[:, :, k * P:(k + 1) * P], Wd.rearrange("(a p) f -> p a f", p=P)[:, :, k * P:(k + 1) * P]).then_inc(ld_wd[k], 16)
            sp.dma_start(wp_raw, Wp.rearrange("(a p) f -> p a f", p=P)).then_inc(ld_wp, 16)
            sp.wait_ge(zeroed, 1)

            def load_x(n):
                if not runs(n, 0):
                    return
                wait(sp, x_turned, n)
                for half in range(2):
                    rows = x[bass.ds(2 * n + half, 1), 0:2 * S, :].rearrange("a (t j) d -> (a t) (j d)", j=2)
                    for a, b in ((0, 48), (48, S)):
                        sp.dma_start(x_sb[HALF * half + a:HALF * half + b, :], rows[a:b, :]).then_inc(x_loaded, 16)

            load_x(0)
            for row in (HALF, HALF + 32):
                sp.dma_start(bias_raw[row:row + 1, 0:F2D], bd.rearrange("(a d) -> a d", a=1)).then_inc(ld_bias, 16)
                sp.dma_start(bias_raw[row:row + 1, F2D:], bp.rearrange("(a d) -> a d", a=1)).then_inc(ld_bias, 16)
            sp.dma_start(b1_raw[0:EXPERTS * KT, :], b1.rearrange("e (f p) -> (e f) p", p=P)).then_inc(ld_b1, 16)
            for src, dst, done in ((Wk, wk_raw, ld_kv), (Wv, wv_raw, ld_kv), (Wdown, wdown, ld_down)):
                d = dst if len(dst.shape) == 3 else dst.rearrange("p (a b) -> p a b", a=KD)
                sp.dma_start(d[:, :, :], src.rearrange("(a p) f -> p a f", p=P)).then_inc(done, 16)
                if done is ld_down:
                    load_x(1)
            sp.dma_start(gamma_b[:, :], gamma.partition_broadcast(P)).then_inc(ld_small, 16)
            sp.dma_start(beta_b[:, :], beta.partition_broadcast(P)).then_inc(ld_small, 16)
            sp.dma_start(wu_b[:, :], Wu.rearrange("d o -> (d o)").partition_broadcast(P)).then_inc(ld_small, 16)
            sp.dma_start(neg_bu[:, :], bu.partition_broadcast(P)).then_inc(ld_small, 16)
            sp.dma_start(decay[:, :], c_decay).then_inc(ld_small, 16)
            sp.dma_start(headmask[:, :], c_headmask).then_inc(ld_small, 16)
            sp.dma_start(gate[:, :], c_gate).then_inc(ld_small, 16)
            sp.dma_start(b2_b[:, :, :].rearrange("p e d -> p (e d)"), b2.rearrange("e d -> (e d)").partition_broadcast(P)).then_inc(ld_small, 16)
            for src, dst in ((Wq, wq), (Wo, wo_raw)):
                d = dst if len(dst.shape) == 3 else dst.rearrange("p (a b) -> p a b", a=KD)
                sp.dma_start(d[:, :, :], src.rearrange("(a p) f -> p a f", p=P)).then_inc(ld_att, 16)
            sp.dma_start(wupk[:, :], Wupk).then_inc(ld_up, 16)
            sp.dma_start(wupv_raw, Wupv).then_inc(ld_up, 16)
            sp.dma_start(we_raw0.rearrange("p (k f) -> p k f", k=KD), W1[0].rearrange("(k p) f -> p k f", p=P)).then_inc(ld_we0, 16)

            def step(m, j, n):
                if not isinstance(n, int) or n > 1:
                    load_x(n)
                if isinstance(n, int) and n == 3:
                    sp.wait_ge(we0_lo, PARTS // 2)
                    sp.dma_start(we_raw0.rearrange("p (k f) -> p k f", k=KT), W2[0].rearrange("(k p) f -> p k f", p=P)).then_inc(ld_we0, 16)

            steps(sp, step)
            sp.wait_ge(y_sum, TILES)
            for e in range(1, EXPERTS):
                if e > 1:
                    sp.wait_ge(we_lo_ok, CHUNKS * (e - 1))
                sp.dma_start(we_raw[:, 0:WCOLS].rearrange("p (k f) -> p k f", k=KD), W1[e].rearrange("(k p) f -> p k f", p=P)).then_inc(ld_we, 16)
                sp.dma_start(we_raw[:, WCOLS:].rearrange("p (k f) -> p k f", k=KT), W2[e].rearrange("(k p) f -> p k f", p=P)).then_inc(ld_we, 16)
            with sp.Fori(0, CHUNKS) as c:
                sp.wait_ge(y_added, c * TPC + TPC * ((EXPERTS - 1) * CHUNKS + 1))
                sp.wait_ge(b2_added, c * TPC + TPC * ((EXPERTS - 1) * CHUNKS + 1))
                o = out.rearrange("(c j h) t d -> c h t j d", j=TPC, h=2)[bass.ds(c, 1)].rearrange("c h t j d -> (c h) t j d")
                r = resid[:, bass.ds(TPC * c, TPC), :]
                for half in range(2):
                    for a, b in ((0, 48), (48, S)):
                        sp.dma_start(o[half, a:b], r[HALF * half + a:HALF * half + b, :, :]).then_inc(stored, 16)
            sp.wait_ge(stored, 16 * 4 * CHUNKS)

        @block.gpsimd
        def _(pool):
            nc.gpsimd.memset(x_sb[:, :], 0.0).then_inc(zeroed, 1)
            nc.gpsimd.memset(halves[:, :].bitcast(F32), 0.0).then_inc(zeroed, 1)
            nc.gpsimd.memset(ones[:, :].bitcast(F32), 1.0).then_inc(zeroed, 1)
            nc.gpsimd.memset(neg_half[:, :], -0.5).then_inc(zeroed, 1)
            nc.gpsimd.memset(eps[:, :], LN_EPS).then_inc(zeroed, 1)
            nc.gpsimd.memset(probs[:, :, :], 0.0).then_inc(zeroed, 1)
            nc.gpsimd.memset(q_bd[:, :, :], 0.0).then_inc(zeroed, 1)
            nc.gpsimd.memset(v_bd[:, :, :, :, :], 0.0).then_inc(zeroed, 1)
            for ha in (ha_hi, ha_lo):
                nc.gpsimd.memset(ha[:, :, S:].bitcast(F32), 0.0).then_inc(h_pad, 1)
            pool.wait_ge(h_pad, 2)

            def rstd(n, mv, mv_ok, ve, ve_ok, r, r_ok):
                wait(pool, mv_ok, n, 1)
                nc.gpsimd.tensor_tensor(ve[:, :], mv[:, 1:2], eps[:, :], ALU.add).then_inc(ve_ok, 1)
                wait(pool, ve_ok, n, 1)
                nc.gpsimd.tensor_tensor(r[:, :], ve[:, :], neg_half[:, :], ALU.pow).then_inc(r_ok, 1)

            def pause():
                nc.gpsimd.tensor_tensor(tick[:, :], eps[:, :], eps[:, :], ALU.add)

            def step(m, j, n):
                if isinstance(n, int) and n == 1:
                    pool.wait_ge(ld_small, N_SMALL * 16)
                if runs(n, 1):
                    h = tile_rows(n - 1)
                    wait(pool, y_normed, n - 1, 1)
                    pause()
                    nc.gpsimd.tensor_tensor(h, h, gamma_b[:, :], ALU.mult).then_inc(y_scaled, 1)
                    wait(pool, y_scaled, n - 1, 1)
                    pause()
                    nc.gpsimd.tensor_tensor(h, h, beta_b[:, :], ALU.add).then_inc(h0_ok, 1)
                if runs(n, 4):
                    rstd(n - 4, h1_mv, h1_mv_ok, h1_ve, h1_ve_ok, h1_rstd, h1_rstd_ok)
                if runs(n, 1):
                    rstd(n - 1, h0_mv, h0_mv_ok, h0_ve, h0_ve_ok, h0_rstd, h0_rstd_ok)
                if isinstance(n, int) and n == 1:
                    pool.wait_ge(wov_hi, 2)
                    nc.gpsimd.tensor_tensor(wo_lo[:, :, :].rearrange("p a b -> p (a b)"), wo_raw,
                                            wo_hi[:, :, :].rearrange("p a b -> p (a b)").bitcast(F32), ALU.subtract).then_inc(wov_lo, 1)
                    nc.gpsimd.tensor_tensor(wupv_lo[:, :], wupv_raw, wupv_hi[:, :].bitcast(F32), ALU.subtract).then_inc(wov_lo, 1)
                    pool.wait_ge(wov_lo, 2)
                for i in parts_in(n):
                    pool.wait_ge(we0_hi, i + 1)
                    nc.gpsimd.tensor_tensor(we_lo[0][:, part0(i)], raw_part(i), we_hi[0][:, part0(i)].bitcast(F32),
                                            ALU.subtract).then_inc(we0_lo, 1)
                if runs(n, 0):
                    rstd(n, y_mv, y_mv_ok, y_ve, y_ve_ok, y_rstd, y_rstd_ok)
                if runs(n, 1):
                    wait(pool, k_cp_ok, n - 1, 1)
                    wait(pool, sc_sum, n - 1)
                    nc.gpsimd.tensor_tensor(
                        k_exp[:, :, :, :],
                        k_cp[:, :, :].unsqueeze(2).broadcast_to([P, QUADS, HPQ, S]),
                        headmask[:, :].unsqueeze(1).unsqueeze(3).broadcast_to([P, QUADS, HPQ, S]),
                        ALU.mult).then_inc(k_exp_ok, 1)
                    wait(pool, latT_hi_ok, n - 1, 1)
                    nc.gpsimd.tensor_tensor(latT_lo[:, :], latT[:, :], latT_hi[:, :].bitcast(F32), ALU.subtract).then_inc(latT_lo_ok, 1)
                    wait(pool, latT_lo_ok, n - 1, 1)

            steps(pool, step)
            pool.wait_ge(at_sum, TILES)
            for h in (h_hi, h_lo):
                nc.gpsimd.memset(h[:, :, :, S:].bitcast(F32), 0.0).then_inc(h_pad, 1)
            for e in range(1, EXPERTS):
                with pool.Fori(0, CHUNKS) as c:
                    part = bass.ds(PREP * c, PREP)
                    pool.wait_ge(we_hi_ok, c + (CHUNKS * (e - 1) + 1))
                    nc.gpsimd.tensor_tensor(we_lo[e % 2][:, part], we_raw[:, part],
                                            we_hi[e % 2][:, part].bitcast(F32), ALU.subtract).then_inc(we_lo_ok, 1)

        @block.scalar
        def _(act):
            for k in range(KF):
                act.wait_ge(setup_pe, k + 1)
                nc.scalar.activation(wdT_hi[:, k, :], psum[:, k, :], ACT.Copy).then_inc(setup_hi, 1)

            def split_wp():
                act.wait_ge(zeroed, 8)
                act.wait_ge(ld_bias, 64)
                for row in (HALF, HALF + 32):
                    nc.scalar.activation(halves[row:row + 1, :], bias_raw[row:row + 1, :], ACT.Copy).then_inc(bias_h, 1)
                for k in range(KF // 2):
                    act.wait_ge(setup_pe, KF + k + 1)
                    nc.scalar.activation(wpT_hi[:, 2 * k:2 * k + 2, :].rearrange("p a d -> p (a d)"), psum[:, wp_bank[k], :], ACT.Copy).then_inc(setup_hi, 1)

            def copy_wkv():
                act.wait_ge(setup_pe, N_SPLIT + 1)
                nc.scalar.activation(wkvT[:, :, :].rearrange("p a b -> p (a b)"), psum[:, 6, :], ACT.Copy).then_inc(setup_hi, 1)
                nc.scalar.activation(b1T[:, :], psum[:, 7, 0:EXPERTS * KT], ACT.Copy).then_inc(setup_hi, 1)

            def copy_wkvd():
                act.wait_ge(setup_pe, N_SPLIT + 2)
                nc.scalar.activation(wkvd[:, :, :].rearrange("p a b -> p (a b)"), psum[:, 7, 128:128 + KD * LAT], ACT.Copy).then_inc(setup_hi, 1)

            def hidden_relu(e, g, f, bank):
                act.wait_ge(f1_sum, g * KT + (f + 1))
                nc.scalar.activation(psum[:, bank, 0:CW], psum[:, bank, 0:CW], ACT.Relu,
                                     bias=b1T[:, e * KT + f:e * KT + f + 1]).then_inc(h_ok, 1)

            def hidden_hi(g, f, bank, hi, used):
                act.wait_ge(h_ok, g * KT + (f + 1))
                if not isinstance(used, int) or used > 0:
                    act.wait_ge(f2_sum, used)
                nc.scalar.activation(hi[:, :, 0:S], clips_of(bank), ACT.Copy).then_inc(h_hi_ok, 1)

            def input_hi(n):
                if not runs(n, 4):
                    return
                wait(act, xn2_turned, n - 4, 1)
                nc.scalar.activation(
                    x2_hi[:, :, bass.ds(ROWS * (n - 4), ROWS)].rearrange("p k (b t) -> p k b t", b=2),
                    ps_x2T.rearrange("p (k b t) -> p k b t", k=KD, b=2)[:, :, :, 0:S], ACT.Copy).then_inc(x2_hi_ok, 1)

            def gate_exp(c):
                act.wait_ge(logit_ok, c * TPC + TPC)
                nc.scalar.activation(u_exp[:, :], logit[:, :], ACT.Exp, bias=neg_bu[:, 0:1], scale=-1.0).then_inc(g_exp, 1)

            def step(m, j, n):
                if j == 0 and older(m, 2):
                    gate_exp(m - 2)
                if runs(n, 0):
                    wait(act, x_turned, n, 1)
                    wait(act, y_sum, n)
                    nc.scalar.activation(xT_hi[:, :, :], ps_xT, ACT.Copy).then_inc(xT_hi_ok, 1)
                if isinstance(n, int) and n == 0:
                    split_wp()
                if ffn_in_window(m):
                    hidden_relu(0, m - 2, 2 * j, bk_f[0])
                if isinstance(n, int) and n == 1:
                    act.wait_ge(ld_att, 32)
                    act.wait_ge(ld_up, 32)
                    nc.scalar.activation(wo_hi[:, :, :].rearrange("p a b -> p (a b)"), wo_raw, ACT.Copy).then_inc(wov_hi, 1)
                    nc.scalar.activation(wupv_hi[:, :], wupv_raw, ACT.Copy).then_inc(wov_hi, 1)
                for i in parts_in(n):
                    act.wait_ge(ld_we0, 16 if i < PARTS // 2 else 32)
                    nc.scalar.activation(we_hi[0][:, part0(i)], raw_part(i), ACT.Copy).then_inc(we0_hi, 1)
                if ffn_in_window(m):
                    hidden_hi(m - 2, 2 * j, bk_f[0], ha_hi, (m - 2) * KT + 2 * j)
                if runs(n, 0):
                    wait(act, hid_sum, n, 1)
                    wait(act, hid_turned, n)
                    nc.scalar.activation(hid[:, :], ps_h, ACT.Tanh).then_inc(hid_ok, 1)
                if isinstance(n, int) and n == 0:
                    copy_wkv()
                if drains(m) and j == 0:
                    act.wait_ge(y_sum, TILES)
                if ffn_in_window(m):
                    hidden_relu(0, m - 2, 2 * j + 1, bank_of(m, 2 * j + 1))
                if not drains(m):
                    input_hi(n)
                if ffn_in_window(m):
                    hidden_hi(m - 2, 2 * j + 1, bank_of(m, 2 * j + 1), hidden_of(m, 2 * j + 1)[0],
                              (m - 2) * KT + (2 * j + (0 if drains(m) else 1)))
                if drains(m):
                    input_hi(n)
                if runs(n, 1):
                    wait(act, xn_turned, n - 1, 1)
                    wait(act, q_sum, n - 1)
                    nc.scalar.activation(xnT[:, :, :].rearrange("p k c -> p (k c)"), ps_xnT, ACT.Copy).then_inc(xnT_ok, 1)
                if runs(n, 0):
                    wait(act, hid_turned, n, 1)
                    nc.scalar.activation(xT_hi[:, :, :], ps_hT, ACT.Copy).then_inc(hidT_hi_ok, 1)
                if isinstance(n, int) and n == 0:
                    copy_wkvd()
                if runs(n, 2):
                    wait(act, sc_shifted, n - 2, 1)
                    nc.scalar.activation(probs[:, :, 0:S], probs[:, :, 0:S], ACT.Exp).then_inc(probs_ok, 1)
                if runs(n, 2):
                    wait(act, v_sum, n - 2, 1)
                    wait(act, pv_sum, n - 2)
                    pv = ps_v.rearrange("p (h e d) -> p h e d", h=HEADS // 2, e=2)
                    for clip in range(2):
                        for par in range(2):
                            last = nc.scalar.activation(
                                v_bd[HALF * par:HALF * (par + 1), :, clip, par, :],
                                pv[HALF * clip:HALF * (clip + 1), :, par, :], ACT.Copy)
                    last.then_inc(v_ok, 1)
                if runs(n, 3):
                    wait(act, o_turned, n - 3, 1)
                    wait(act, at_sum, n - 3)
                    nc.scalar.activation(oT_hi[:, :, :].rearrange("p k c -> p (k c)"), ps_oT, ACT.Copy).then_inc(oT_ok, 1)
                if runs(n, 1):
                    wait(act, lat_sum, n - 1, 1)
                    wait(act, v_sum, n - 1)
                    wait(act, k_sum, n - 1)
                    wait(act, latT_lo_ok, n - 1)
                    nc.scalar.activation(latT[:, :], ps_lat, ACT.Copy).then_inc(lat_ok, 1)
                    wait(act, lat_ok, n - 1, 1)
                    nc.scalar.activation(latT_hi[:, :], latT[:, :], ACT.Copy).then_inc(latT_hi_ok, 1)
                if runs(n, 1):
                    wait(act, k_sum, n - 1, 1)
                    wait(act, k_exp_ok, n - 1)
                    for odd in range(2):
                        for clip in range(2):
                            last = nc.scalar.activation(
                                k_cp[HALF * clip:HALF * (clip + 1), odd::2, :],
                                ps_k[HALF * odd:HALF * (odd + 1), :, HALF * clip:HALF * clip + S], ACT.Copy)
                    last.then_inc(k_cp_ok, 1)
                    wait(act, q_sum, n - 1, 1)
                    wait(act, sc_sum, n - 1)
                    for odd in range(2):
                        for clip in range(2):
                            last = nc.scalar.activation(
                                q_bd[HALF * clip:HALF * (clip + 1), odd::2, HALF * clip:HALF * (clip + 1)],
                                ps_q[HALF * odd:HALF * (odd + 1), :, HALF * clip:HALF * (clip + 1)], ACT.Copy)
                    last.then_inc(q_ok, 1)
                if isinstance(n, int) and n == 2:
                    act.wait_ge(wov_lo, 2)
                if runs(n, 2):
                    wait(act, p_turned, n - 2, 1)
                    wait(act, pv_sum, n - 2)
                    for b in range(2):
                        last = nc.scalar.activation(pT[:, 4 * b:4 * b + 4, :].rearrange("p h q -> p (h q)"),
                                                    ps_pT[:, b, :], ACT.Copy)
                    last.then_inc(pT_ok, 1)

            steps(act, step)
            gate_exp(CHUNKS - 1)
            act.wait_ge(at_sum, TILES)
            act.wait_ge(xn2_turned, TILES)

            def split_next(e, c):
                part = bass.ds(PREP * c, PREP)
                act.wait_ge(ld_we, 32 * (e + 1))
                if e:
                    act.wait_ge(f2_sum, KT * CHUNKS * e)
                nc.scalar.activation(we_hi[(e + 1) % 2][:, part], we_raw[:, part], ACT.Copy).then_inc(we_hi_ok, 1)

            def chunk(e, c):
                g = c + CHUNKS * e
                for f in range(KT):
                    bank = bk_f[f % 3]
                    hidden_relu(e, g, f, bank)
                    hidden_hi(g, f, bank, h_hi[:, f % 4, :, :], g * KT + (f - 3) if f >= 4 or e else 0)
                    if e == 0:
                        split_next(0, f)
                    if f == KT - 3 and 0 < e < EXPERTS - 1:
                        split_next(e, c)

            chunks(act, chunk)

        @block.vector
        def _(dve):
            for k in range(KF):
                dve.wait_ge(setup_hi, k + 1)
                nc.vector.tensor_tensor(wdT_lo[:, k, :], psum[:, k, :], wdT_hi[:, k, :].bitcast(F32), ALU.subtract).then_inc(setup_lo, 1)

            def split_wp():
                dve.wait_ge(bias_h, 2)
                row = halves[HALF + 32:HALF + 33, :]
                nc.vector.tensor_tensor(row, bias_raw[HALF + 32:HALF + 33, :], row.bitcast(F32), ALU.subtract).then_inc(bias_done, 1)
                for k in range(KF // 2):
                    dve.wait_ge(setup_hi, KF + k + 1)
                    nc.vector.tensor_tensor(wpT_lo[:, 2 * k:2 * k + 2, :].rearrange("p a d -> p (a d)"), psum[:, wp_bank[k], :],
                                            wpT_hi[:, 2 * k:2 * k + 2, :].rearrange("p a d -> p (a d)").bitcast(F32), ALU.subtract).then_inc(setup_lo, 1)
                dve.wait_ge(ld_kv, 32)
                nc.vector.tensor_tensor(wkv[:, :, :].rearrange("p a b -> p (a b)"), wk_raw, wv_raw, ALU.add).then_inc(wkv_sum, 1)

            def hidden_lo(g, f, bank, hi, lo):
                dve.wait_ge(h_hi_ok, g * KT + (f + 1))
                nc.vector.tensor_tensor(lo[:, :, 0:S], clips_of(bank), hi[:, :, 0:S].bitcast(F32), ALU.subtract).then_inc(h_lo_ok, 1)

            def weight(e, t):
                return w_gate[:, e, :][:, bass.ds(t, 1)]

            def add_output(e, c, g):
                dve.wait_ge(b2_added, g * TPC + TPC)
                dve.wait_ge(f2_sum, g * KT + KT)
                for j in range(TPC):
                    t = tile_rows(c * TPC + j)
                    nc.vector.scalar_tensor_tensor(out=t, in0=ps_e[:, j, :], scalar=weight(e, c * TPC + j), in1=t,
                                                   op0=ALU.mult, op1=ALU.add).then_inc(y_added, 1)

            def add_bias(e, t, g):
                if not isinstance(g, int) or g > 0:
                    dve.wait_ge(y_added, g * TPC)
                nc.vector.scalar_tensor_tensor(out=tile_rows(t), in0=b2_b[:, e, :], scalar=weight(e, t), in1=tile_rows(t),
                                               op0=ALU.mult, op1=ALU.add).then_inc(b2_added, 1)

            def gate_weights(c):
                dve.wait_ge(g_exp, c + 1)
                nc.vector.tensor_scalar(u_den[:, :], u_exp[:, :], 1.0, None, ALU.add).then_inc(g_step, 1)
                dve.wait_ge(g_step, c * 3 + 2)
                nc.vector.reciprocal(u[:, :], u_den[:, :]).then_inc(g_step, 1)
                dve.wait_ge(g_step, c * 3 + 3)
                for e in range(EXPERTS):
                    last = nc.vector.tensor_scalar(w_step[:, e, :], u[:, :], gate[:, e:e + 1],
                                                   gate[:, EXPERTS + e:EXPERTS + e + 1], ALU.is_gt, ALU.mult)
                last.then_inc(g_step, 1)
                dve.wait_ge(g_step, c * 3 + 4)
                nc.vector.tensor_tensor(w_gate[:, :, bass.ds(c * TPC, TPC)], w_step[:, :, :],
                                        u[:, :].unsqueeze(1).broadcast_to([P, EXPERTS, TPC]), ALU.mult).then_inc(w_ok, 1)

            def own_columns(n):
                if not runs(n, 3):
                    return
                wait(dve, pv_sum, n - 3, 1)
                wait(dve, inv_ok, n - 3, 1)
                wait(dve, o_turned, n - 3)
                for clip in range(2):
                    rows = slice(HALF * clip, HALF * (clip + 1))
                    last = nc.vector.tensor_tensor(
                        o_sb[rows, :, :].rearrange("p (h e) d -> p h e d", e=2), ps_pv[rows, :, clip, :, :],
                        row_inv[rows, :].rearrange("p (h e) -> p h e", e=2).unsqueeze(3).broadcast_to([HALF, HEADS // 2, 2, DH]),
                        ALU.mult)
                last.then_inc(o_ok, 1)

            def step(m, j, n):
                if isinstance(n, int) and n == 1:
                    dve.wait_ge(ld_small, N_SMALL * 16)
                    nc.vector.tensor_scalar(neg_bu[:, :], neg_bu[:, :], -1.0, None, ALU.mult).then_inc(g_step, 1)
                if runs(n, 1):
                    wait(dve, y_rstd_ok, n - 1, 1)
                    if isinstance(n, int) and n == 1:
                        dve.wait_ge(setup_hi, N_SPLIT + 3)
                        dve.wait_ge(setup_pe, N_SPLIT + 2)
                    nc.vector.tensor_scalar(tile_rows(n - 1), ps_y, y_mv[:, 0:1], y_rstd[:, 0:1],
                                            ALU.subtract, ALU.mult).then_inc(y_normed, 1)
                if runs(n, 4):
                    wait(dve, h1_ok, n - 4, 1)
                if runs(n, 0):
                    wait(dve, xT_hi_ok, n, 1)
                    nc.vector.tensor_tensor(xT_lo[:, :, :], ps_xT, xT_hi[:, :, :].bitcast(F32), ALU.subtract).then_inc(xT_lo_ok, 1)
                if isinstance(n, int) and n == 0:
                    split_wp()
                if runs(n, 4):
                    nc.vector.bn_stats(h1_stats[:, :], tile_rows(n - 4)).then_inc(h1_st_ok, 1)
                    wait(dve, h1_st_ok, n - 4, 1)
                if ffn_in_window(m):
                    hidden_lo(m - 2, 2 * j, bk_f[0], ha_hi, ha_lo)
                if runs(n, 4):
                    nc.vector.bn_aggr(h1_mv[:, :], h1_stats[:, :]).then_inc(h1_mv_ok, 1)
                if runs(n, 2):
                    wait(dve, sc_sum, n - 2, 1)
                    nc.vector.tensor_scalar(ps_sc, ps_sc, -CLAMP * SCALE_INV, CLAMP * SCALE_INV,
                                            ALU.max, ALU.min).then_inc(sc_clipped, 1)
                if runs(n, 1):
                    wait(dve, h0_ok, n - 1, 1)
                if runs(n, 4):
                    wait(dve, h1_rstd_ok, n - 4, 1)
                    wait(dve, logit_ok, n - 4)
                    nc.vector.tensor_scalar(xn2[:, :], tile_rows(n - 4), h1_mv[:, 0:1], h1_rstd[:, 0:1],
                                            ALU.subtract, ALU.mult).then_inc(xn2_ok, 1)
                if runs(n, 1):
                    nc.vector.bn_stats(h0_stats[:, :], tile_rows(n - 1)).then_inc(h0_st_ok, 1)
                    wait(dve, h0_st_ok, n - 1, 1)
                if runs(n, 2):
                    wait(dve, sc_clipped, n - 2, 1)
                    nc.vector.tensor_tensor(ps_sc_h, ps_sc_h,
                                            decay[:, :].unsqueeze(1).unsqueeze(1).broadcast_to([P, 2, 2 * HPQ, S]),
                                            ALU.mult).then_inc(sc_decayed, 1)
                if runs(n, 1):
                    nc.vector.bn_aggr(h0_mv[:, :], h0_stats[:, :]).then_inc(h0_mv_ok, 1)
                if runs(n, 2):
                    wait(dve, sc_decayed, n - 2, 1)
                    nc.vector.tensor_reduce(row_max[:, :].rearrange("p (b h) -> p b h", b=2), ps_sc_h, AX.X, ALU.max).then_inc(max_ok, 1)
                if runs(n, 1):
                    wait(dve, h0_rstd_ok, n - 1, 1)
                    wait(dve, xn_turned, n - 1)
                    nc.vector.tensor_scalar(xn[:, :], tile_rows(n - 1), h0_mv[:, 0:1], h0_rstd[:, 0:1],
                                            ALU.subtract, ALU.mult).then_inc(xn_ok, 1)
                if drains(m):
                    if not runs(n, 2):
                        own_columns(n)
                    hidden_lo(m - 2, 2 * j + 1, bank_of(m, 2 * j + 1), *hidden_of(m, 2 * j + 1))
                if runs(n, 4):
                    wait(dve, x2_hi_ok, n - 4, 1)
                    cols = bass.ds(ROWS * (n - 4), ROWS)
                    nc.vector.tensor_tensor(
                        x2_lo[:, :, cols].rearrange("p k (b t) -> p k b t", b=2),
                        ps_x2T.rearrange("p (k b t) -> p k b t", k=KD, b=2)[:, :, :, 0:S],
                        x2_hi[:, :, cols].rearrange("p k (b t) -> p k b t", b=2).bitcast(F32),
                        ALU.subtract).then_inc(x2_lo_ok, 1)
                if runs(n, 2):
                    wait(dve, max_ok, n - 2, 1)
                    wait(dve, p_turned, n - 2)
                    nc.vector.tensor_tensor(
                        probs[:, :, 0:S].rearrange("p (b h) k -> p b h k", b=2), ps_sc_h,
                        row_max[:, :].rearrange("p (b h) -> p b h", b=2).unsqueeze(3).broadcast_to([P, 2, 2 * HPQ, S]),
                        ALU.subtract).then_inc(sc_shifted, 1)
                if ffn_in_window(m) and not drains(m):
                    hidden_lo(m - 2, 2 * j + 1, bk_f[0], ha_hi, ha_lo)
                if runs(n, 2):
                    own_columns(n)
                if runs(n, 0):
                    wait(dve, hidT_hi_ok, n, 1)
                    nc.vector.tensor_tensor(xT_lo[:, :, :], ps_hT, xT_hi[:, :, :].bitcast(F32), ALU.subtract).then_inc(hidT_lo_ok, 1)
                if runs(n, 4):
                    wait(dve, xn2_ok, n - 4, 1)
                    if j == 0 and older(m, 2):
                        dve.wait_ge(g_exp, m - 1)
                    wait(dve, xn2_turned, n - 4, 1)
                    nc.vector.tensor_tensor_reduce(xn2[:, :], xn2[:, :], wu_b[:, :], 1.0, 0.0, ALU.mult, ALU.add,
                                                   logit[:, j:j + 1]).then_inc(logit_ok, 1)
                if j > 0 and ffn_in_window(m):
                    add_bias(0, (m - 2) * TPC + j, m - 2)
                if runs(n, 2):
                    wait(dve, probs_ok, n - 2, 1)
                    nc.vector.tensor_reduce(row_sum[:, :], probs[:, :, 0:S], AX.X, ALU.add).then_inc(sum_ok, 1)
                if runs(n, 3):
                    wait(dve, oT_ok, n - 3, 1)
                    nc.vector.tensor_tensor(oT_lo[:, :, :].rearrange("p k c -> p (k c)"), ps_oT,
                                            oT_hi[:, :, :].rearrange("p k c -> p (k c)").bitcast(F32), ALU.subtract).then_inc(oT_lo_ok, 1)
                if runs(n, 0):
                    wait(dve, y_sum, n, 1)
                    nc.vector.bn_stats(y_stats[:, :], ps_y).then_inc(y_st_ok, 1)
                    wait(dve, y_st_ok, n, 1)
                if runs(n, 2):
                    wait(dve, sum_ok, n - 2, 1)
                    nc.vector.reciprocal(row_inv[:, :], row_sum[:, :]).then_inc(inv_ok, 1)
                if runs(n, 0):
                    nc.vector.bn_aggr(y_mv[:, :], y_stats[:, :]).then_inc(y_mv_ok, 1)
                if j == 0 and ffn_in_window(m):
                    gate_weights(m - 2)
                    dve.wait_ge(w_ok, m - 1)
                    add_bias(0, (m - 2) * TPC + j, m - 2)
                if j == TPC - 1 and ffn_in_window(m):
                    add_output(0, m - 2, m - 2)
                if runs(n, 3):
                    wait(dve, at_sum, n - 3, 1)
                    nc.vector.tensor_tensor(tile_rows(n - 3), ps_at, tile_rows(n - 3), ALU.add).then_inc(h1_ok, 1)

            steps(dve, step)
            dve.wait_ge(at_sum, TILES)
            dve.wait_ge(xn2_turned, TILES)

            def chunk(e, c):
                g = c + CHUNKS * e
                if e:
                    first = isinstance(c, int)
                    add_output(e - 1 if first else e, CHUNKS - 1 if first else c - 1, g - 1)
                for f in range(KT):
                    hidden_lo(g, f, bk_f[f % 3], h_hi[:, f % 4, :, :], h_lo[:, f % 4, :, :])
                    if e == 0 and f == 2:
                        gate_weights(CHUNKS - 1)
                        dve.wait_ge(w_ok, CHUNKS)
                    if f >= TPC:
                        add_bias(e, c * TPC + (f - TPC), g)

            chunks(dve, chunk)
            add_output(EXPERTS - 1, CHUNKS - 1, CHUNKS * EXPERTS - 1)

        @block.tensor
        def _(pe):
            pe.wait_ge(ld_ident, 16)
            for k in range(KF):
                pe.wait_ge(ld_wd[k], 16)
                for g in range(KF):
                    last = nc.tensor.transpose(psum[:, k, g * P:(g + 1) * P], wd_raw[:, g, k * P:(k + 1) * P], ident[:, :])
                last.then_inc(setup_pe, 1)

            def turn_wp():
                pe.wait_ge(ld_wp, 16)
                for k2 in range(KF // 2):
                    for i in range(2):
                        for d in range(KD):
                            k = 2 * k2 + i
                            last = nc.tensor.transpose(psum[:, wp_bank[k2], (KD * i + d) * P:(KD * i + d + 1) * P],
                                                       wp_raw[:, d, k * P:(k + 1) * P], ident[:, :])
                    last.then_inc(setup_pe, 1)

            def turn_wkv():
                pe.wait_ge(setup_lo, N_SPLIT)
                pe.wait_ge(wkv_sum, 1)
                pe.wait_ge(ld_b1, 16)
                for j in range(KD):
                    for i in range(KD):
                        nc.tensor.transpose(psum[:, 6, (KD * j + i) * P:(KD * j + i + 1) * P], wkv[:, i, j * P:(j + 1) * P], ident[:, :])
                nb = EXPERTS * KT
                nc.tensor.transpose(psum[:, 7, 0:nb], b1_raw[0:nb, :], ident[0:nb, 0:nb]).then_inc(setup_pe, 1)

            def project_wkv():
                pe.wait_ge(setup_hi, N_SPLIT + 2)
                pe.wait_ge(ld_down, 16)
                for i in range(KD):
                    for j in range(KD):
                        last = nc.tensor.matmul(psum[:, 7, 128 + i * LAT:128 + (i + 1) * LAT], wkvT[:, j, i * P:(i + 1) * P],
                                                wdown[:, j, :], start=(j == 0), stop=(j == KD - 1))
                last.then_inc(setup_pe, 1)

            def split_product(dst, lhs_hi, lhs_lo, rhs_hi, rhs_lo, first, last):
                nc.tensor.matmul(dst, lhs_hi, rhs_hi, start=first, stop=False)
                nc.tensor.matmul(dst, lhs_hi, rhs_lo, start=False, stop=False)
                return nc.tensor.matmul(dst, lhs_lo, rhs_hi, start=False, stop=last)

            def first_layer(e, g, c, f, bank, free):
                if not isinstance(free, int) or free > 0:
                    pe.wait_ge(h_lo_ok, free)
                w_hi = we_hi[e % 2][:, 0:WCOLS].rearrange("p (k f) -> p k f", k=KD)
                w_lo = we_lo[e % 2][:, 0:WCOLS].rearrange("p (k f) -> p k f", k=KD)
                cols, feats = bass.ds(c * CW, CW), slice(f * P, (f + 1) * P)
                for k in range(KD):
                    last = split_product(psum[:, bank, 0:CW], w_hi[:, k, feats], w_lo[:, k, feats],
                                         x2_hi[:, k, cols], x2_lo[:, k, cols], k == 0, k == KD - 1)
                last.then_inc(f1_sum, 1)

            def rows_of(h, j):
                return h[:, 2 * j:2 * j + 2, :].rearrange("p b t -> p (b t)")

            def second_layer(e, g, f, hi, lo):
                pe.wait_ge(h_lo_ok, g * KT + (f + 1))
                if f == 0 and (not isinstance(g, int) or g > 0):
                    pe.wait_ge(y_added, g * TPC)
                w_hi = we_hi[e % 2][:, WCOLS:].rearrange("p (k d) -> p k d", k=KT)
                w_lo = we_lo[e % 2][:, WCOLS:].rearrange("p (k d) -> p k d", k=KT)
                for j in range(TPC):
                    last = split_product(ps_e[:, j, :], rows_of(hi, j), rows_of(lo, j), w_hi[:, f, :], w_lo[:, f, :],
                                         f == 0 and j % 2 == 0, f == KT - 1 and j % 2 == 1)
                last.then_inc(f2_sum, 1)

            def probs_v(n):
                if not runs(n, 3):
                    return
                wait(pe, pT_ok, n - 3, 1)
                wait(pe, v_ok, n - 3, 1)
                wait(pe, h1_ok, n - 4, 1)
                for h in range(HEADS // 2):
                    last = nc.tensor.matmul(ps_pv[:, h, :, :, :].rearrange("p b e d -> p (b e d)"), pT[:, h, :],
                                            v_bd[:, h, :, :, :].rearrange("p b e d -> p (b e d)"), start=True, stop=True)
                last.then_inc(pv_sum, 1)

            def turn_heads(n):
                if not runs(n, 3):
                    return
                wait(pe, o_ok, n - 3, 1)
                for k in range(KD):
                    last = nc.tensor.transpose(ps_oT[:, k * P:(k + 1) * P],
                                               o_sb[:, k * P // DH:(k + 1) * P // DH, :].rearrange("p h d -> p (h d)"), ident[:, :])
                last.then_inc(o_turned, 1)

            def turn_input(n):
                if not runs(n, 4):
                    return
                wait(pe, xn2_ok, n - 4, 1)
                if runs(n, 0):
                    wait(pe, xT_lo_ok, n, 1)
                for k in range(KD):
                    last = nc.tensor.transpose(ps_x2T[:, k * P:(k + 1) * P], xn2[:, k * P:(k + 1) * P], ident[:, :])
                last.then_inc(xn2_turned, 1)

            def step(m, j, n):
                ffn, g = ffn_in_window(m), m - 2
                if isinstance(n, int) and n == 2:
                    pe.wait_ge(wov_lo, 2)
                if runs(n, 0):
                    wait(pe, x_loaded, n, 1, 64)
                    wait(pe, q_ok, n - 1)
                    for k in range(KF):
                        last = nc.tensor.transpose(ps_xT[:, k, :], x_sb[:, k * P:(k + 1) * P], ident[:, :])
                    last.then_inc(x_turned, 1)
                if isinstance(n, int) and n == 0:
                    turn_wp()
                    pe.wait_ge(setup_lo, KF)
                if ffn:
                    if isinstance(m, int) and m == 2 and j == 0:
                        pe.wait_ge(we0_lo, PARTS)
                        pe.wait_ge(h_pad, 2)
                    first_layer(0, g, g, 2 * j, bk_f[0], g * KT + 2 * j)
                if runs(n, 2):
                    wait(pe, q_ok, n - 2, 1)
                    wait(pe, k_exp_ok, n - 2, 1)
                    if runs(n, 3):
                        wait(pe, pT_ok, n - 3, 1)
                    for c in range(QUADS):
                        last = nc.tensor.matmul(ps_sc[:, c // 2, (c % 2) * HPQ * S:(c % 2 + 1) * HPQ * S], q_bd[:, c, :],
                                                k_exp[:, c, :, :].rearrange("p h k -> p (h k)"), start=True, stop=True)
                    last.then_inc(sc_sum, 1)
                if runs(n, 0):
                    wait(pe, xT_lo_ok, n, 1)
                    wait(pe, y_normed, n)
                    for k in range(KF):
                        split_product(ps_h, xT_hi[:, k, :], xT_lo[:, k, :], wdT_hi[:, k, :], wdT_lo[:, k, :], k == 0, False)
                    if isinstance(n, int) and n == 0:
                        pe.wait_ge(bias_h, 2)
                        pe.wait_ge(bias_done, 1)
                    nc.tensor.matmul(ps_h, ones[HALF:P, :], bias2[:, 0:F2D], start=False, stop=True).then_inc(hid_sum, 1)
                if isinstance(n, int) and n == 0:
                    turn_wkv()
                if ffn:
                    if drains(m) and j == 0:
                        pe.wait_ge(y_normed, TILES)
                    first_layer(0, g, g, 2 * j + 1, bank_of(m, 2 * j + 1), g * KT + (2 * j + (0 if drains(m) else 1)))
                if drains(m):
                    probs_v(n)
                    second_layer(0, g, 2 * j, ha_hi, ha_lo)
                    turn_input(n)
                    if not runs(n, 2):
                        turn_heads(n)
                if not drains(m):
                    turn_input(n)
                if ffn and not drains(m):
                    second_layer(0, g, 2 * j, ha_hi, ha_lo)
                if not drains(m):
                    probs_v(n)
                if isinstance(n, int) and n == 1:
                    pe.wait_ge(setup_hi, N_SPLIT + 3)
                    pe.wait_ge(ld_att, 32)
                    pe.wait_ge(ld_up, 32)
                if runs(n, 1):
                    wait(pe, xn_ok, n - 1, 1)
                    if runs(n, 4):
                        wait(pe, x2_lo_ok, n - 4, 1)
                    elif runs(n, 0):
                        wait(pe, xT_lo_ok, n, 1)
                    for k in range(KD):
                        last = nc.tensor.transpose(ps_xnT[:, k * P:(k + 1) * P], xn[:, k * P:(k + 1) * P], ident[:, :])
                    last.then_inc(xn_turned, 1)
                if runs(n, 0):
                    wait(pe, hid_ok, n, 1)
                    for k in range(KF):
                        last = nc.tensor.transpose(ps_hT[:, k, :], hid[:, k * P:(k + 1) * P], ident[:, :])
                    last.then_inc(hid_turned, 1)
                if isinstance(n, int) and n == 0:
                    project_wkv()
                if ffn:
                    second_layer(0, g, 2 * j + 1, *hidden_of(m, 2 * j + 1))
                if runs(n, 2):
                    wait(pe, lat_ok, n - 2, 1)
                    wait(pe, sc_shifted, n - 2, 1)
                    wait(pe, latT_lo_ok, n - 2, 1)
                    split_product(ps_v, latT_hi[:, :], latT_lo[:, :], wupv_hi[:, :], wupv_lo[:, :], True, True).then_inc(v_sum, 1)
                if runs(n, 1):
                    wait(pe, xnT_ok, n - 1, 1)
                    for k in range(KD):
                        last = nc.tensor.matmul(ps_lat, wkvd[:, k, :], xnT[:, k, :], start=(k == 0), stop=(k == KD - 1))
                    last.then_inc(lat_sum, 1)
                if not drains(m) or runs(n, 2):
                    turn_heads(n)
                if runs(n, 0):
                    wait(pe, hidT_lo_ok, n, 1)
                    nc.tensor.matmul(ps_y, ones[HALF:P, :], bias2[:, F2D:], start=True, stop=False)
                    for k in range(KF):
                        last = split_product(ps_y, xT_hi[:, k, :], xT_lo[:, k, :], wpT_hi[:, k, :], wpT_lo[:, k, :],
                                             False, k == KF - 1)
                    last.then_inc(y_sum, 1)
                if runs(n, 1):
                    wait(pe, lat_ok, n - 1, 1)
                    wait(pe, v_ok, n - 2, 1)
                    for q in range(KD):
                        last = nc.tensor.matmul(ps_k[:, q, :], wupk[:, q * P:(q + 1) * P], latT[:, :], start=True, stop=True)
                    last.then_inc(k_sum, 1)
                    for q in range(KD):
                        for k in range(KD):
                            last = nc.tensor.matmul(ps_q[:, q, :], wq[:, k, q * P:(q + 1) * P], xnT[:, k, :],
                                                    start=(k == 0), stop=(k == KD - 1))
                    last.then_inc(q_sum, 1)
                if runs(n, 2):
                    wait(pe, probs_ok, n - 2, 1)
                    wait(pe, lat_ok, n - 1, 1)
                    wait(pe, v_ok, n - 2, 1)
                    for h in range(HEADS // 2):
                        if h == HPQ:
                            wait(pe, k_cp_ok, n - 1, 1)
                        last = nc.tensor.transpose(ps_pT[:, h // 4, (h % 4) * P:(h % 4 + 1) * P],
                                                   probs[:, 2 * h:2 * h + 2, :].rearrange("p e k -> p (e k)"), ident[:, :])
                    last.then_inc(p_turned, 1)
                if runs(n, 3):
                    wait(pe, oT_lo_ok, n - 3, 1)
                    for k in range(KD):
                        last = split_product(ps_at, oT_hi[:, k, :], oT_lo[:, k, :], wo_hi[:, k, :], wo_lo[:, k, :], k == 0, k == KD - 1)
                    last.then_inc(at_sum, 1)

            steps(pe, step)
            pe.wait_ge(h1_ok, TILES)
            pe.wait_ge(x2_lo_ok, TILES)
            pe.wait_ge(y_normed, TILES)
            pe.wait_ge(h_pad, 4)

            def chunk(e, c):
                g = c + CHUNKS * e
                if e:
                    pe.wait_ge(we_lo_ok, CHUNKS * e)
                for f in range(3):
                    first_layer(e, g, c, f, bk_f[f], g * KT)
                for f in range(KT):
                    second_layer(e, g, f, h_hi[:, f % 4, :, :], h_lo[:, f % 4, :, :])
                    if f + 3 < KT:
                        first_layer(e, g, c, f + 3, bk_f[f % 3], g * KT + (f + 1))

            chunks(pe, chunk)


_INS = ['x', 'L0_tok_Wd', 'L0_tok_bd', 'L0_tok_Wp', 'L0_tok_bp', 'L0_tok_gamma', 'L0_tok_beta', 'L0_attn_Wq',
        'L0_attn_Wk', 'L0_attn_Wv', 'L0_attn_Wo', 'L0_attn_W_down_kv', 'L0_attn_W_up_k', 'L0_attn_W_up_v',
        'L0_ffn_W1', 'L0_ffn_b1', 'L0_ffn_W2', 'L0_ffn_b2', 'L0_ffn_Wu', 'L0_ffn_bu']
_OUT = (CLIPS, S, D)


def constants():
    import numpy as np
    row = np.arange(P) % HALF
    decay = np.exp(np.float32(-0.01 * 0.01) * np.abs(row[:, None] - np.arange(S)[None, :]).astype(np.float32))
    headmask = (row[:, None] // DH == np.arange(HPQ)[None, :]).astype(np.float32)
    step = (np.arange(EXPERTS)[None, :] - row[:, None]) % EXPERTS + 1
    gate = np.concatenate([np.where(step == 1, -1.0, (step - 1) / EXPERTS), 1.0 / step], axis=1)
    return {"c_ident": np.eye(P, dtype=np.float32), "c_decay": (decay / np.float32(SCALE_INV)).astype(np.float32),
            "c_headmask": headmask, "c_gate": gate.astype(np.float32)}


def kernel(**inputs):
    import numpy as _np
    import concourse.bacc as _bacc
    from concourse import mybir as _mybir
    from concourse.bass_utils import run_bass_kernel_spmd as _run

    nc = _bacc.Bacc("TRN2", target_bir_lowering=False, num_devices=1)
    arrays, args = {}, []
    tables = constants()
    for name in _INS + list(tables):
        a = _np.ascontiguousarray(tables[name] if name in tables else inputs[name])
        arrays[f"in_{name}_dram"] = a
        args.append(nc.dram_tensor(f"in_{name}_dram", a.shape, _mybir.dt.from_np(a.dtype), kind="ExternalInput").ap())
    args.append(nc.dram_tensor("out_0_dram", _OUT, F32, kind="ExternalOutput").ap())
    build(nc, *args)
    r = _run(nc, [arrays], core_ids=[0])
    return r.results[0]["out_0_dram"]
```
